# Optimizing a Trainium2 kernel written in Bass

```python
import numpy as np
import jax
import jax.numpy as jnp

def _softmax(x, axis=-1):
    return jax.nn.softmax(x, axis=axis)

def _gelu(x):
    return jax.nn.gelu(x, approximate=True)

def _silu(x):
    return jax.nn.silu(x)

def _sigmoid(x):
    return jax.nn.sigmoid(x)

def _layernorm(x, axis=-1, eps=1e-05):
    m = jnp.mean(x, axis=axis, keepdims=True)
    v = jnp.var(x, axis=axis, keepdims=True)
    return (x - m) / jnp.sqrt(v + eps)

def _scatter_add(tgt, idx, src, axis=0):
    return tgt.at[idx].add(src)

def _segment_sum(src, seg, n):
    return jax.ops.segment_sum(src, seg, n)
kernel_name = 'mk_xattn_ffn_d1_seqx_r4_c67632'

def setup_inputs(seed: int=0):
    np.random.seed(seed)
    _w = jnp.asarray

    def _rec_inputs():
        import jax
        import jax.numpy as jnp
        _rk = jax.random.key(seed)
        x = 0.0003765 + 1 * jax.random.normal(jax.random.fold_in(_rk, 1), (8, 256, 512), jnp.float32)
        _lenS = 256 - jax.random.randint(jax.random.fold_in(_rk, 7), (8,), 0, max(1, 256 // 4) + 1, jnp.int32)
        _lenS2 = 256 - jax.random.randint(jax.random.fold_in(_rk, 8), (8,), 0, max(1, 256 // 4) + 1, jnp.int32)
        _ctx_2048P = jax.random.normal(jax.random.fold_in(_rk, 11), (8, 16, 512), jnp.float32)
        _ctx_2048c = jax.random.dirichlet(jax.random.fold_in(_rk, 511), 0.3 * jnp.ones((16,), jnp.float32), (8, 256))
        _ctx_2048t = jnp.einsum('bsk,bkd->bsd', _ctx_2048c, _ctx_2048P)
        _ctx_2048t = _ctx_2048t * jax.lax.rsqrt(jnp.mean(jnp.square(_ctx_2048t)) + 1e-12) * 0.953939
        ctx_2048 = -0.000292821 + 1.00034 * (_ctx_2048t + 0.3 * jax.random.normal(jax.random.fold_in(_rk, 611), (8, 256, 512), jnp.float32))
        return (x, ctx_2048)
    x, ctx_2048 = _rec_inputs()

    def _L0_xattn_setup():
        import jax, jax.numpy as jnp
        import numpy as np
        key = jax.random.key(seed)
        k1, k2, k3, k4, k5 = jax.random.split(key, 5)
        B, D_MODEL, L = (2, 256, 512)
        HEAD_DIM = 8
        H = D_MODEL // HEAD_DIM
        return {'k': jax.random.normal(k1, (B, D_MODEL, L), dtype=jnp.float32), 'v': jax.random.normal(k2, (B, D_MODEL, L), dtype=jnp.float32), 'q': jax.random.normal(k3, (B, D_MODEL, L), dtype=jnp.float32), 'ssm_kernel': jax.random.normal(k4, (H, L), dtype=jnp.float32), 'D': jax.random.normal(k5, (H,), dtype=jnp.float32), 'head_dim': HEAD_DIM}
    _L0_xattn_all = _L0_xattn_setup()
    _L0_xattn_in = {k: v for k, v in _L0_xattn_all.items() if k in ('ssm_kernel', 'D')}
    del _L0_xattn_all

    def _L0_ffn_setup():
        import jax, jax.numpy as jnp
        import numpy as np
        DIM = 512
        INNER = 2048
        EPS_RMS = 1e-06
        EPS_Q = 1e-05

        def simple_rms_norm(x, dim):
            rms = jnp.sqrt(jnp.mean(x * x, axis=-1, keepdims=True) + EPS_RMS)
            return x / rms * dim ** (-0.5)

        def activation_quant(x):
            scale = 127.0 / jnp.clip(jnp.max(jnp.abs(x), axis=-1, keepdims=True), EPS_Q)
            return jnp.clip(jnp.round(x * scale), -128, 127) / scale

        def weight_quant(w):
            return jnp.sign(w) * jnp.mean(jnp.abs(w))

        def bit_linear(x, w, b, dim_in):
            x_norm = simple_rms_norm(x, dim_in)
            x_q = activation_quant(x_norm)
            w_q = weight_quant(w)
            return jnp.einsum('bsd,od->bso', x_q, w_q) + b
        key = jax.random.key(seed)
        k1, k2, k3, k4, k5 = jax.random.split(key, 5)
        bound1 = 1.0 / np.sqrt(DIM)
        bound2 = 1.0 / np.sqrt(INNER)
        return {'x': jax.random.normal(k1, (4, 512, DIM), dtype=jnp.float32), 'w1': jax.random.uniform(k2, (INNER, DIM), jnp.float32, -bound1, bound1), 'b1': jax.random.uniform(k3, (INNER,), jnp.float32, -bound1, bound1), 'w2': jax.random.uniform(k4, (DIM, INNER), jnp.float32, -bound2, bound2), 'b2': jax.random.uniform(k5, (DIM,), jnp.float32, -bound2, bound2)}
    _L0_ffn_all = _L0_ffn_setup()
    _L0_ffn_in = {k: v for k, v in _L0_ffn_all.items() if k in ('w1', 'b1', 'w2', 'b2')}
    del _L0_ffn_all
    return {'x': x, 'ctx_2048': ctx_2048, 'L0_xattn_ssm_kernel': _L0_xattn_in['ssm_kernel'], 'L0_xattn_D': _L0_xattn_in['D'], 'L0_ffn_w1': _L0_ffn_in['w1'], 'L0_ffn_b1': _L0_ffn_in['b1'], 'L0_ffn_w2': _L0_ffn_in['w2'], 'L0_ffn_b2': _L0_ffn_in['b2']}

def reference(x, ctx_2048, L0_xattn_ssm_kernel, L0_xattn_D, L0_ffn_w1, L0_ffn_b1, L0_ffn_w2, L0_ffn_b2):
    import jax
    import jax.numpy as jnp

    def _L0_xattn_ref(k, v, q, ssm_kernel, D, head_dim):
        import jax, jax.numpy as jnp
        import numpy as np
        B, HD, L = k.shape
        H = HD // head_dim
        fft_size = 2 * L
        k_ = k.reshape(B, H, head_dim, L)
        v_ = v.reshape(B, H, head_dim, L)
        q_ = q.reshape(B, H, head_dim, L)
        kv = jnp.einsum('bhil,bhjl->bijhl', k_, v_)
        kv_f = jnp.fft.rfft(kv, n=fft_size)
        kernel_f = jnp.fft.rfft(ssm_kernel, n=fft_size)
        y = jnp.fft.irfft(kv_f * kernel_f, n=fft_size)[..., :L]
        out = y + kv * D[None, None, None, :, None]
        out = jnp.einsum('bijhl,bhil->bjhl', out, q_)
        out = jnp.transpose(out, (0, 2, 1, 3)).reshape(B, H * head_dim, L)
        return out.astype(k.dtype)

    def _L0_ffn_ref(x, w1, b1, w2, b2):
        import jax, jax.numpy as jnp
        import numpy as np
        DIM = 512
        INNER = 2048
        EPS_RMS = 1e-06
        EPS_Q = 1e-05

        def simple_rms_norm(x, dim):
            rms = jnp.sqrt(jnp.mean(x * x, axis=-1, keepdims=True) + EPS_RMS)
            return x / rms * dim ** (-0.5)

        def activation_quant(x):
            scale = 127.0 / jnp.clip(jnp.max(jnp.abs(x), axis=-1, keepdims=True), EPS_Q)
            return jnp.clip(jnp.round(x * scale), -128, 127) / scale

        def weight_quant(w):
            return jnp.sign(w) * jnp.mean(jnp.abs(w))

        def bit_linear(x, w, b, dim_in):
            x_norm = simple_rms_norm(x, dim_in)
            x_q = activation_quant(x_norm)
            w_q = weight_quant(w)
            return jnp.einsum('bsd,od->bso', x_q, w_q) + b
        h = bit_linear(x, w1, b1, DIM)
        h = jax.nn.gelu(h, approximate=False)
        return bit_linear(h, w2, b2, INNER)
    x = x + _L0_xattn_ref(ctx_2048, ctx_2048, _layernorm(x, axis=-1), L0_xattn_ssm_kernel, L0_xattn_D, 8)
    x = x + _L0_ffn_ref(_layernorm(x, axis=-1), L0_ffn_w1, L0_ffn_b1, L0_ffn_w2, L0_ffn_b2)
    return x

_drawn_inputs = setup_inputs


def setup_inputs(seed=0):
    import zlib

    import numpy as np

    out = dict(_drawn_inputs(seed))
    spreads = {}
    factors = {'L0_ffn_w1': 200.0, 'L0_ffn_b1': 200.0, 'L0_ffn_w2': 200.0, 'L0_ffn_b2': 200.0}
    for name, (base, spread) in spreads.items():
        noise = np.random.default_rng([zlib.crc32(name.encode()), seed]).standard_normal(out[name].shape)
        drawn = base * np.exp(spread * noise) if base else spread * noise
        out[name] = jnp.asarray(drawn.astype(out[name].dtype))
    for name, factor in factors.items():
        out[name] = (out[name] * factor).astype(out[name].dtype)
    return out
```

```python
from contextlib import ExitStack

import concourse.bass as bass
from concourse import mybir

F32 = mybir.dt.float32
F32R = mybir.dt.float32r
BF16 = mybir.dt.bfloat16
ALU = mybir.AluOpType
ACT = mybir.ActivationFunctionType
AX = mybir.AxisListType

P = 128
MAGIC = 1.5 * 2.0**23
TINY = 1e-20


def view(tensor, offset, dims):
    whole = tensor[:]
    return bass.AP(tensor=whole.tensor, offset=whole.offset + offset,
                   ap=[list(whole.ap[0])] + [list(d) for d in dims])


def build(nc, x, ctx, ssm_kernel, D, w1, b1, w2, b2, out):
    B, CH, L = x.shape
    H = ssm_kernel.shape[0]
    HD = CH // H
    INNER = w1.shape[0]
    LB = L // P
    KB = INNER // P
    NCH = INNER // L
    HALF = HD // 2
    PART = HALF * B * HALF
    NPR = 3 * PART
    ROWS = 2 * HD
    TILES = CH // ROWS
    BAND = L + P
    assert ROWS * B == P and B == HD and L == 512 and TILES % 2 == 0 and NPR <= 512

    def rows_of(ap, t):
        return ap.rearrange("b (t r) d -> t r b d", r=ROWS)[bass.ds(t, 1)]

    kern_dram = nc.dram_tensor("kern_reversed", (2, H, BAND), F32, kind="Internal").ap()

    with ExitStack() as stack:
        def sb(name, shape, dt=F32):
            return stack.enter_context(nc.sbuf_tensor(name, shape, dt))

        def two(name, shape, dt=F32):
            return [sb(f"{name}{i}", shape, dt) for i in range(2)]

        def sem(name):
            return stack.enter_context(nc.semaphore(name))

        def sem2(name):
            return [sem(f"{name}{i}") for i in range(2)]

        ident = sb("ident", [P, P])
        ident_bf = sb("ident_bf", [P, P], BF16)
        ones = sb("ones", [P, P])
        magic = sb("magic", [P, 1])
        minus_half = sb("minus_half", [P, 1])
        inner_eps = sb("inner_eps", [P, 1])
        w1s = sb("w1s", [P, LB, INNER], BF16)
        w2s = sb("w2s", [P, KB, L], BF16)
        bias_rows = sb("bias_rows", [P, INNER], BF16)
        b2_all = sb("b2_all", [P, L])
        kern_rev = sb("kern_rev", [H, BAND])
        D_col = sb("D_col", [H, 1])
        abs_sums = sb("abs_sums", [P, 2, 16])
        abs_sum = sb("abs_sum", [P, 2])
        w_mean = sb("w_mean", [P, 2])
        w_mean_inv = sb("w_mean_inv", [P, 2])

        band = two("band", [P, 2, 2, L], F32R)
        x_in = two("x_in", [P, L])
        c_in = two("c_in", [P, L])
        x_res = two("x_res", [P, L])
        q_rev = sb("q_rev", [P, L])
        c_nat = sb("c_nat", [P, LB * P])
        c_bat = sb("c_bat", [P, LB * P])
        prod = sb("prod", [P, LB, 2, NPR])
        prod_hi = two("prod_hi", [P, LB, 2, NPR], F32R)
        prod_lo = two("prod_lo", [P, LB, 2, NPR], F32R)
        q_t = two("q_t", [P, LB, P])
        z = sb("z", [P, 2, LB, HD, HD * B])
        z4 = sb("z4", [P, LB, HD // 2, HD * B])
        z2 = sb("z2", [P, LB, HD // 4, HD * B])
        attn_t = two("attn_t", [P, LB, P])
        x1 = two("x1", [P, L])
        x1_b2 = two("x1_b2", [P, L])
        cent = sb("cent", [P, L])
        xq = sb("xq", [P, L + P], BF16)
        xq_t = sb("xq_t", [P, LB + 1, P], BF16)
        g = sb("g", [P, INNER])
        square_dump = sb("square_dump", [P, INNER], BF16)
        gq = sb("gq", [P, INNER], BF16)
        gq_t = sb("gq_t", [P, KB, P], BF16)
        y_out = two("y_out", [P, L])
        stats1_buf = sb("stats1_buf", [P, nc.vector.BN_STATS_DIM])
        stats2_buf = sb("stats2_buf", [P, nc.vector.BN_STATS_DIM])
        mv1 = two("mv1", [P, 2])
        var1 = two("var1", [P, 1])
        rstd1 = two("rstd1", [P, 1])
        mv2 = two("mv2", [P, 2])
        cmax = two("cmax", [P, 1])
        var2 = two("var2", [P, 1])
        norm1 = two("norm1", [P, 1])
        norm2 = two("norm2", [P, 1])
        biggest = sb("biggest", [P, 2])
        to_int1 = two("to_int1", [P, 1])
        to_int2 = two("to_int2", [P, 1])
        unit1 = two("unit1", [P, 1])
        unit2 = two("unit2", [P, 1])
        per_unit1 = two("per_unit1", [P, 3])
        gsum = two("gsum", [P, 1])
        gmax = two("gmax", [P, 1])
        spare = prod_hi[1][0:H].rearrange("p a b c -> p (a b c)")
        kern_hi = spare[:, 0:BAND]
        kern_lo = spare[:, BAND:2 * BAND]
        w_stage = [view(z, i * L, [[1, L]]) for i in range(4)]
        w_sign = [gq[:, i * L:(i + 1) * L] for i in range(4)]
        b1_f32 = g
        b1_part = [z[:].rearrange("p a b c d -> p (a b c d)")[:, 2048:3072].bitcast(BF16),
                   z[:].rearrange("p a b c d -> p (a b c d)")[:, 3072:4096].bitcast(BF16),
                   z4[:].rearrange("p b c d -> p (b c d)")[:, 0:1024].bitcast(BF16)]

        ps_y = [stack.enter_context(nc.psum_tensor(f"ps_y{i}", [P, L], F32)) for i in range(LB)]
        w_bank = [bank[:].bitcast(BF16)[:, 0:L] for bank in ps_y]
        ps_t = stack.enter_context(nc.psum_tensor("ps_t", [P, L], F32))
        ps_b = stack.enter_context(nc.psum_tensor("ps_b", [P, 2 * L], BF16))
        ps_f = [stack.enter_context(nc.psum_tensor(f"ps_f{i}", [P, L], F32)) for i in range(2)]

        consts_set = sem("consts_set")
        pads_set = sem("pads_set")
        kern_in = sem("kern_in")
        kern_step = sem("kern_step")
        kern_split = sem("kern_split")
        kern_stored = sem("kern_stored")
        b1_in = sem("b1_in")
        b1_step = sem("b1_step")
        bias_in = sem("bias_in")
        b2_in = sem("b2_in")
        w_in = [sem(f"w_in{i}") for i in range(4)]
        w_signed = sem("w_signed")
        w_summed = sem("w_summed")
        w_turned = sem("w_turned")
        w_placed = sem("w_placed")
        w_total = sem("w_total")
        w_mean_step = sem("w_mean_step")
        w_mean_ready = sem("w_mean_ready")

        x_loaded = sem2("x_loaded")
        c_loaded = sem2("c_loaded")
        res_loaded = sem2("res_loaded")
        band_loaded = sem2("band_loaded")
        stored = sem2("stored")
        stats1_ready = sem("stats1_ready")
        mv1_step = sem("mv1_step")
        mv1_ready = sem("mv1_ready")
        rstd1_ready = sem("rstd1_ready")
        q_ready = sem("q_ready")
        q_turned = sem("q_turned")
        q_t_ready = sem("q_t_ready")
        c_turned = sem("c_turned")
        c_t_ready = sem("c_t_ready")
        prod_ready = sem("prod_ready")
        hi_ready = sem("hi_ready")
        lo_ready = sem("lo_ready")
        conv_ready = sem("conv_ready")
        z_ready = sem("z_ready")
        sum_step = sem("sum_step")
        attn_ready = sem("attn_ready")
        attn_turned = sem("attn_turned")
        x1_ready = sem("x1_ready")
        x1_b2_ready = sem("x1_b2_ready")
        stats2_ready = sem("stats2_ready")
        mv2_step = sem("mv2_step")
        cmax_ready = sem("cmax_ready")
        var2_ready = sem("var2_ready")
        norm1_ready = sem("norm1_ready")
        scale1_step = sem("scale1_step")
        to_int1_ready = sem("to_int1_ready")
        unit1_ready = sem("unit1_ready")
        per_unit1_ready = sem("per_unit1_ready")
        factor_step = sem("factor_step")
        factors_ready = sem("factors_ready")
        xq_step = sem("xq_step")
        xq_ready = sem("xq_ready")
        xq_turned = sem("xq_turned")
        xq_t_ready = sem("xq_t_ready")
        first_ready = sem("first_ready")
        g_ready = sem("g_ready")
        gsum_ready = sem("gsum_ready")
        gmax_ready = sem("gmax_ready")
        gsum_step = sem("gsum_step")
        norm2_ready = sem("norm2_ready")
        scale2_step = sem("scale2_step")
        to_int2_ready = sem("to_int2_ready")
        unit2_ready = sem("unit2_ready")
        g_rounded = sem("g_rounded")
        gq_ready = sem("gq_ready")
        gq_turned = sem("gq_turned")
        gq_t_ready = sem("gq_t_ready")
        second_ready = sem("second_ready")
        y_ready = sem("y_ready")

        block = stack.enter_context(nc.Block())

        def pipeline(eng, iteration):
            iteration(0, 0, True, True, False, False)
            iteration(0, 1, True, True, True, False)
            iteration(1, 0, True, True, True, True)
            iteration(1, 1, True, True, True, True)
            with eng.Fori(2, TILES // 2 - 1) as j:
                iteration(j, 0, True, True, True, True)
                iteration(j, 1, True, True, True, True)
            iteration(TILES // 2 - 1, 0, True, True, True, True)
            iteration(TILES // 2 - 1, 1, False, True, True, True)
            iteration(TILES // 2, 0, False, False, True, True)
            iteration(TILES // 2, 1, False, False, False, True)

        def before(j, p, n):
            pair, parity = j - (n - p + 1) // 2, (p - n) % 2
            return pair, parity, 2 * pair + parity

        @block.sync
        def _(sp):
            def load_x_and_c(j, p, waits=True):
                t = 2 * j + p
                if waits:
                    sp.wait_ge(q_ready, t - 1)
                sp.dma_start(x_in[p][:], rows_of(x, t)).then_inc(x_loaded[p], 16)
                if waits:
                    sp.wait_ge(c_turned, t - 1)
                sp.dma_start(c_in[p][:], rows_of(ctx, t)).then_inc(c_loaded[p], 16)

            def load_band(j, p, waits=True):
                t = 2 * j + p
                if waits:
                    sp.wait_ge(conv_ready, 2 * LB * (t - 1))
                for part in range(2):
                    whole = kern_dram[part]
                    src = bass.AP(tensor=whole.tensor, offset=whole.offset + 2 * BAND * t,
                                  ap=[[1, P], [BAND, 2], [1, L]])
                    sp.dma_start(band[p][:, part].bitcast(F32), src).then_inc(band_loaded[p], 16)

            def load_residual(j, p, waits=True):
                t = 2 * j + p
                if waits:
                    sp.wait_ge(x1_ready, t - 1)
                sp.dma_start(x_res[p][:], rows_of(x, t)).then_inc(res_loaded[p], 16)

            def store(j, p):
                sp.wait_ge(y_ready, 2 * j + p + 1)
                sp.dma_start(rows_of(out, 2 * j + p), y_out[p][:]).then_inc(stored[p], 16)

            load_x_and_c(0, 0, False)
            sp.dma_start(cent[0:H, :], ssm_kernel).then_inc(kern_in, 16)
            sp.dma_start(D_col[:], D.rearrange("(h a) -> h a", a=1)).then_inc(kern_in, 16)
            sp.dma_start(b1_f32[0:3, :], b1.rearrange("(a n) -> a n", a=1).to_broadcast([3, INNER])
                         ).then_inc(b1_in, 16)
            load_x_and_c(0, 1, False)
            sp.wait_ge(kern_split, 2)
            sp.dma_start(kern_dram[0], kern_hi.bitcast(F32)).then_inc(kern_stored, 16)
            sp.dma_start(kern_dram[1], kern_lo.bitcast(F32)).then_inc(kern_stored, 16)
            sp.dma_start(b2_all[:], b2.rearrange("(a n) -> a n", a=1).to_broadcast([P, L])
                         ).then_inc(b2_in, 16)

            w1_rows = w1.rearrange("(u p) n -> u p n", p=P)
            w2_rows = w2.rearrange("(r p) (c n) -> r c p n", p=P, n=L)
            def load_weights(j, matrix):
                for s in range(4):
                    if matrix or not isinstance(j, int):
                        sp.wait_ge(w_signed, 4 * j + 16 * matrix)
                        sp.wait_ge(w_summed, 4 * j + 16 * matrix)
                    src = w2_rows[bass.ds(j, 1), s] if matrix else w1_rows[bass.ds(4 * j + s, 1)]
                    sp.dma_start(w_stage[s], src).then_inc(w_in[s], 16)

            load_weights(0, 0)
            with sp.Fori(1, 4) as j:
                load_weights(j, 0)
            with sp.Fori(0, 4) as j:
                load_weights(j, 1)
            sp.wait_ge(kern_stored, 32)
            load_band(0, 0, False)
            load_band(0, 1, False)
            load_residual(0, 0, False)
            load_residual(0, 1, False)
            sp.wait_ge(b1_step, 5)
            sp.wait_ge(pads_set, 5)
            for part in range(3):
                sp.dma_start(bias_rows[part:9:3, :], b1_part[part][0:3, :]).then_inc(bias_in, 16)

            def iteration(j, p, prepare, convolve, first, second):
                if prepare and not (isinstance(j, int) and 2 * j + p == TILES - 2):
                    load_x_and_c(j + 1, p)
                if first and convolve:
                    pair, parity, _ = before(j, p, -1)
                    if not (isinstance(j, int) and 2 * j + p == TILES - 1):
                        load_band(pair, parity)
                        load_residual(pair, parity)
                if second and not (isinstance(j, int) and 2 * j + p == 2):
                    pair, parity, _ = before(j, p, 3)
                    store(pair, parity)

            iteration(0, 0, True, True, False, False)
            iteration(0, 1, True, True, True, False)
            iteration(1, 0, True, True, True, True)
            iteration(1, 1, True, True, True, True)
            with sp.Fori(2, TILES // 2 - 1) as j:
                iteration(j, 0, True, True, True, True)
                iteration(j, 1, True, True, True, True)
            iteration(TILES // 2 - 1, 0, True, True, True, True)
            iteration(TILES // 2 - 1, 1, False, True, True, True)
            iteration(TILES // 2, 0, False, False, True, True)
            iteration(TILES // 2, 1, False, False, False, True)
            store(TILES // 2 - 1, 1)
            for p in range(2):
                sp.wait_ge(stored[p], 16 * TILES // 2)

        @block.tensor
        def _(pe):
            def turn_c(j, p):
                t = 2 * j + p
                pe.wait_ge(c_loaded[p], 16 * j + 16)
                pe.wait_ge(q_t_ready, t)
                for lb in range(LB):
                    last = nc.tensor.transpose(ps_t[:, lb * P:(lb + 1) * P],
                                               c_in[p][:, lb * P:(lb + 1) * P], ident[:])
                last.then_inc(c_turned, 1)

            def turn_q(j, p, others):
                t = 2 * j + p
                pe.wait_ge(q_ready, t + 1)
                pe.wait_ge(c_t_ready, 2 * t + 2)
                if others:
                    pe.wait_ge(x1_ready, t - 1)
                for lb in range(LB):
                    last = nc.tensor.transpose(ps_t[:, lb * P:(lb + 1) * P],
                                               q_rev[:, lb * P:(lb + 1) * P], ident[:])
                last.then_inc(q_turned, 1)

            def convolve_head(j, p, head):
                t = 2 * j + p
                if head == 0:
                    pe.wait_ge(band_loaded[p], 32 * j + 32)
                for lb in range(LB):
                    if head == 0 and lb % 2 == 0:
                        pe.wait_ge(hi_ready, 2 * t + lb // 2 + 1)
                        pe.wait_ge(lo_ready, 2 * t + lb // 2 + 1)
                    if head == 1 or not (isinstance(j, int) and t == 0):
                        pe.wait_ge(z_ready, 2 * LB * t + head * LB + lb - LB + 1)
                    n = 0
                    for mb in range(lb + 1):
                        at = (LB - 1 - (lb - mb)) * P
                        for kpart, ppart in ((0, 0), (0, 1), (1, 0)):
                            src = (prod_hi, prod_lo)[ppart][p]
                            last = nc.tensor.matmul(ps_y[lb][:, 0:NPR],
                                                    band[p][:, kpart, head, at:at + P],
                                                    src[:, mb, head, :],
                                                    start=(n == 0), stop=(n == 3 * lb + 2))
                            n += 1
                    last.then_inc(conv_ready, 1)

            def turn_attention(j, p, others):
                t = 2 * j + p
                pe.wait_ge(attn_ready, 2 * t + 2)
                if others:
                    pe.wait_ge(c_t_ready, 2 * t + 6)
                else:
                    pe.wait_ge(q_t_ready, t + 1)
                for lb in range(LB):
                    last = nc.tensor.transpose(ps_t[:, lb * P:(lb + 1) * P],
                                               attn_t[p][:, lb, :], ident[:])
                last.then_inc(attn_turned, 1)

            def turn_tokens(j, p, others):
                t = 2 * j + p
                pe.wait_ge(xq_ready, t + 1)
                pe.wait_ge(factors_ready, t + 1)
                if others:
                    pe.wait_ge(gq_t_ready, 2 * t)
                for kb in range(LB + 1):
                    last = nc.tensor.transpose(ps_b[:, kb * P:(kb + 1) * P],
                                               xq[:, kb * P:(kb + 1) * P], ident_bf[:])
                last.then_inc(xq_turned, 1)

            def first_product(j, p, others):
                t = 2 * j + p
                pe.wait_ge(xq_t_ready, t + 1)
                for n in range(NCH):
                    bank = ps_f[(p + n) % 2]
                    if n == 0 and others:
                        pe.wait_ge(g_ready, NCH * t)
                    if n == 1 and others:
                        pe.wait_ge(y_ready, t)
                    if n >= 2:
                        pe.wait_ge(g_ready, NCH * t + n - 1)
                    for kb in range(LB):
                        nc.tensor.matmul(bank[:], xq_t[:, kb, :], w1s[:, kb, n * L:(n + 1) * L],
                                         start=(kb == 0), stop=False)
                    nc.tensor.matmul(bank[:], xq_t[:, LB, :], bias_rows[:, n * L:(n + 1) * L],
                                     start=False, stop=True).then_inc(first_ready, 1)

            def turn_g(j, p, half):
                t = 2 * j + p
                if half == 0:
                    pe.wait_ge(gq_ready, t + 1)
                    pe.wait_ge(xq_t_ready, t + 1)
                else:
                    pe.wait_ge(gq_t_ready, 2 * t + 1)
                for k in range(KB // 2):
                    kb = half * KB // 2 + k
                    last = nc.tensor.transpose(ps_b[:, k * P:(k + 1) * P],
                                               gq[:, kb * P:(kb + 1) * P], ident_bf[:])
                last.then_inc(gq_turned, 1)

            def second_product(j, p):
                t = 2 * j + p
                bank = ps_f[p]
                pe.wait_ge(gq_t_ready, 2 * t + 2)
                pe.wait_ge(g_ready, NCH * t + 3)
                for kb in range(KB):
                    last = nc.tensor.matmul(bank[:], gq_t[:, kb, :], w2s[:, kb, :],
                                            start=(kb == 0), stop=(kb == KB - 1))
                last.then_inc(second_ready, 1)

            pe.wait_ge(pads_set, 5)
            turn_c(0, 0)
            turn_q(0, 0, False)
            def turn_weights(j, matrix):
                for s in range(4):
                    pe.wait_ge(w_signed, 4 * j + 16 * matrix + s + 1)
                    if matrix or not isinstance(j, int):
                        pe.wait_ge(w_placed, 4 * j + 16 * matrix)
                    for kb in range(4):
                        last = nc.tensor.transpose(w_bank[s][:, kb * P:(kb + 1) * P],
                                                   w_sign[s][:, kb * P:(kb + 1) * P], ident_bf[:])
                    last.then_inc(w_turned, 1)

            turn_weights(0, 0)
            with pe.Fori(1, 4) as j:
                turn_weights(j, 0)
            with pe.Fori(0, 4) as j:
                turn_weights(j, 1)
            pe.wait_ge(w_total, 1)
            nc.tensor.matmul(ps_f[0][:, 0:2], ones[:], abs_sum[:], start=True, stop=True
                             ).then_inc(w_total, 1)
            pe.wait_ge(w_mean_step, 1)
            pe.wait_ge(bias_in, 48)

            def iteration(j, p, prepare, convolve, first, second):
                now, one, two_, nxt = (before(j, p, n)[:2] for n in (0, 1, 2, -1))
                if prepare:
                    turn_c(*nxt)
                if convolve:
                    convolve_head(*now, 0)
                if first:
                    turn_attention(*one, prepare)
                if convolve:
                    convolve_head(*now, 1)
                if second:
                    turn_g(*two_, 0)
                    turn_g(*two_, 1)
                    second_product(*two_)
                if prepare:
                    turn_q(*nxt, first)
                if first:
                    turn_tokens(*one, second)
                    first_product(*one, second)

            pipeline(pe, iteration)

        @block.scalar
        def _(act):
            def place_c(j, p):
                t = 2 * j + p
                act.wait_ge(c_turned, t + 1)
                act.wait_ge(prod_ready, 4 * t)
                nc.scalar.activation(c_nat[:], ps_t[:], ACT.Copy).then_inc(c_t_ready, 1)
                G = 4 * LB
                nc.scalar.activation(
                    c_bat[:].rearrange("m (g b i) -> m g b i", g=G, b=B),
                    ps_t[:].rearrange("m (g i b) -> m g b i", g=G, b=B), ACT.Copy).then_inc(c_t_ready, 1)

            def place_q(j, p, reuse):
                t = 2 * j + p
                act.wait_ge(q_turned, t + 1)
                if reuse:
                    act.wait_ge(z_ready, 2 * LB * (t - 1))
                nc.scalar.activation(q_t[p][:].rearrange("p a b -> p (a b)"), ps_t[:], ACT.Copy
                                     ).then_inc(q_t_ready, 1)

            def round_products(j, p, half, reuse):
                t = 2 * j + p
                act.wait_ge(prod_ready, 4 * t + 2 * half + 2)
                if half == 0 and reuse:
                    act.wait_ge(conv_ready, 2 * LB * (t - 1))
                nc.scalar.activation(prod_hi[p][:, 2 * half:2 * half + 2], prod[:, 2 * half:2 * half + 2],
                                     ACT.Copy).then_inc(hi_ready, 1)

            def bias_factors(j, p, others):
                t = 2 * j + p
                act.wait_ge(per_unit1_ready, t + 1)
                if others:
                    act.wait_ge(xq_turned, t)
                for part in range(3):
                    left = per_unit1[p][:, part:part + 1]
                    factor = xq[:, L + 3 * part:L + 3 * part + 3]
                    if part < 2:
                        nc.scalar.activation(factor, left.to_broadcast([P, 3]), ACT.Copy).then_inc(factor_step, 1)
                        act.wait_ge(factor_step, 4 * t + 2 * part + 1)
                        nc.scalar.activation(per_unit1[p][:, part + 1:part + 2], factor[:, 0:1], ACT.Identity,
                                             bias=left, scale=-1.0).then_inc(factor_step, 1)
                        act.wait_ge(factor_step, 4 * t + 2 * part + 2)
                    else:
                        nc.scalar.activation(factor, left.to_broadcast([P, 3]), ACT.Copy).then_inc(factors_ready, 1)

            def place_tokens(j, p, others):
                t = 2 * j + p
                act.wait_ge(xq_turned, t + 1)
                if others:
                    act.wait_ge(first_ready, NCH * t)
                nc.scalar.activation(xq_t[:].rearrange("p a b -> p (a b)"), ps_b[:, 0:(LB + 1) * P],
                                     ACT.Copy).then_inc(xq_t_ready, 1)

            def gelu(j, p, others):
                t = 2 * j + p
                if others:
                    act.wait_ge(gq_ready, t)
                act.wait_ge(unit1_ready, t + 1)
                for n in range(NCH):
                    act.wait_ge(first_ready, NCH * t + n + 1)
                    nc.scalar.activation(g[:, n * L:(n + 1) * L], ps_f[(p + n) % 2][:], ACT.Gelu,
                                         scale=unit1[p][:]).then_inc(g_ready, 1)

            def sum_squares(j, p):
                t = 2 * j + p
                act.wait_ge(g_ready, NCH * t + NCH)
                nc.scalar.activation(square_dump[:], g[:], ACT.Square, accum_out=gsum[p][:]
                                     ).then_inc(gsum_ready, 1)

            def round_g(j, p):
                t = 2 * j + p
                act.wait_ge(to_int2_ready, t + 1)
                act.wait_ge(gmax_ready, t + 1)
                act.wait_ge(gsum_ready, t + 1)
                nc.scalar.activation(g[:], g[:], ACT.Identity, bias=magic[:], scale=to_int2[p][:]
                                     ).then_inc(g_rounded, 1)

            def place_g(j, p, half, others):
                t = 2 * j + p
                act.wait_ge(gq_turned, 2 * t + half + 1)
                if half == 0 and others:
                    act.wait_ge(second_ready, t)
                nc.scalar.activation(gq_t[:, half * KB // 2:(half + 1) * KB // 2, :].rearrange("p a b -> p (a b)"),
                                     ps_b[:], ACT.Copy).then_inc(gq_t_ready, 1)

            place_c(0, 0)
            place_q(0, 0, False)
            for half in range(2):
                round_products(0, 0, half, False)
            def sign_weights(j, matrix):
                for s in range(4):
                    act.wait_ge(w_in[s], 16 * j + 64 * matrix + 16)
                    if matrix or not isinstance(j, int):
                        act.wait_ge(w_turned, 4 * j + 16 * matrix)
                    nc.scalar.activation(w_sign[s], w_stage[s], ACT.Sign).then_inc(w_signed, 1)

            sign_weights(0, 0)
            with act.Fori(1, 4) as j:
                sign_weights(j, 0)
            with act.Fori(0, 4) as j:
                sign_weights(j, 1)
            act.wait_ge(kern_stored, 32)

            def iteration(j, p, prepare, convolve, first, second):
                now, one, two_, nxt = (before(j, p, n)[:2] for n in (0, 1, 2, -1))
                if prepare:
                    place_c(*nxt)
                if second:
                    sum_squares(*two_)
                    round_g(*two_)
                if prepare:
                    round_products(*nxt, 0, first)
                    round_products(*nxt, 1, first)
                if second:
                    place_g(*two_, 0, not (isinstance(j, int) and 2 * j + p == 2))
                    place_g(*two_, 1, True)
                if first:
                    bias_factors(*one, second)
                if prepare:
                    place_q(*nxt, first)
                if first:
                    place_tokens(*one, second)
                    gelu(*one, second)

            pipeline(act, iteration)

        @block.gpsimd
        def _(pool):
            pe_ = nc.gpsimd

            def make_rstd1(j, p):
                t = 2 * j + p
                pool.wait_ge(mv1_ready, t + 1)
                pe_.tensor_tensor(rstd1[p][:], var1[p][:], minus_half[:], ALU.pow).then_inc(rstd1_ready, 1)

            def multiply_c(j, p, half):
                t = 2 * j + p
                if half == 0:
                    pool.wait_ge(c_t_ready, 2 * t + 2)
                    pool.wait_ge(hi_ready, 2 * t)
                    pool.wait_ge(lo_ready, 2 * t)
                W = HALF * B
                for part, heads, o1, o2, step, count in ((0, 2, 0, 0, 2 * PART, 2), (1, 1, 0, W, 0, 1)):
                    n = 4 * heads
                    base = half * 2 * P
                    left = view(c_nat, base + o1, [[2 * W // heads, n], [1, W], [0, HALF]])
                    right = view(c_bat, base + o2, [[2 * W // heads, n], [0, HALF], [1, W]])
                    if part == 0:
                        dst = view(prod, half * 4 * NPR, [[NPR, 4], [2 * PART, 2], [1, PART]])
                    else:
                        dst = view(prod, half * 4 * NPR + PART, [[NPR, 4], [1, PART]])
                    pe_.tensor_tensor(dst, left, right, ALU.mult).then_inc(prod_ready, 1)

            def remainders(j, p, half):
                t = 2 * j + p
                pool.wait_ge(hi_ready, 2 * t + half + 1)
                hi = prod_hi[p][:, 2 * half:2 * half + 2].bitcast(F32)
                pe_.tensor_tensor(prod_lo[p][:, 2 * half:2 * half + 2], prod[:, 2 * half:2 * half + 2], hi,
                                  ALU.subtract).then_inc(lo_ready, 1)

            def make_norm1(j, p):
                t = 2 * j + p
                pool.wait_ge(var2_ready, t + 1)
                pe_.tensor_tensor(norm1[p][:], var2[p][:], minus_half[:], ALU.pow).then_inc(norm1_ready, 1)

            def add_b2(j, p, reuse):
                t = 2 * j + p
                pool.wait_ge(x1_ready, t + 1)
                if reuse:
                    pool.wait_ge(y_ready, t - 1)
                pe_.tensor_tensor(x1_b2[p][:], x1[p][:], b2_all[:], ALU.add).then_inc(x1_b2_ready, 1)

            def make_norm2(j, p):
                t = 2 * j + p
                pool.wait_ge(gsum_ready, t + 1)
                pe_.tensor_tensor(gsum[p][:], gsum[p][:], inner_eps[:], ALU.add).then_inc(gsum_step, 1)
                pool.wait_ge(gsum_step, t + 1)
                pe_.tensor_tensor(norm2[p][:], gsum[p][:], minus_half[:], ALU.pow).then_inc(norm2_ready, 1)

            for m, value in ((ident, 0.0), (ones, 1.0), (magic, MAGIC), (minus_half, -0.5),
                             (inner_eps, INNER * 1e-6)):
                pe_.memset(m[:], value).then_inc(consts_set, 1)
            pool.wait_ge(consts_set, 5)
            pe_.affine_select(out=ident[:], in_=ident[:], compare_op=ALU.not_equal, fill=1.0, base=0,
                              pattern=[[-1, P]], channel_multiplier=1).then_inc(pads_set, 1)
            pool.wait_ge(pads_set, 1)
            pe_.tensor_copy(ident_bf[:], ident[:]).then_inc(pads_set, 1)
            pe_.memset(kern_rev[:, L:BAND], 0.0).then_inc(pads_set, 1)
            pe_.memset(bias_rows[:], 0.0).then_inc(pads_set, 1)
            pe_.memset(xq[:], 0.0).then_inc(pads_set, 1)
            make_rstd1(0, 0)
            multiply_c(0, 0, 0)
            multiply_c(0, 0, 1)
            remainders(0, 0, 0)
            remainders(0, 0, 1)
            pool.wait_ge(b2_in, 16)

            def iteration(j, p, prepare, convolve, first, second):
                now, one, two_, nxt = (before(j, p, n)[:2] for n in (0, 1, 2, -1))
                if prepare:
                    make_rstd1(*nxt)
                    multiply_c(*nxt, 0)
                if second:
                    make_norm2(*two_)
                if prepare:
                    multiply_c(*nxt, 1)
                if first:
                    make_norm1(*one)
                if prepare:
                    remainders(*nxt, 0)
                if first:
                    add_b2(*one, not (isinstance(j, int) and 2 * j + p <= 2))
                if prepare:
                    remainders(*nxt, 1)

            pipeline(pool, iteration)

        @block.vector
        def _(dve):
            v = nc.vector

            def stats1(j, p):
                dve.wait_ge(x_loaded[p], 16 * j + 16)
                v.bn_stats(stats1_buf[:], x_in[p][:]).then_inc(stats1_ready, 1)

            def variance1(j, p):
                t = 2 * j + p
                v.bn_aggr(mv1[p][:], stats1_buf[:]).then_inc(mv1_step, 1)
                dve.wait_ge(mv1_step, t + 1)
                v.tensor_scalar(var1[p][:], mv1[p][:, 1:2], 1e-5, None, ALU.add).then_inc(mv1_ready, 1)

            def make_q(j, p):
                t = 2 * j + p
                dve.wait_ge(rstd1_ready, t + 1)
                dve.wait_ge(q_turned, t)
                v.tensor_scalar(view(q_rev, 0, [[P, LB], [1, P]]), view(x_in[p], P - 1, [[P, LB], [-1, P]]),
                                mv1[p][:, 0:1], rstd1[p][:], ALU.subtract, ALU.mult).then_inc(q_ready, 1)

            def multiply_q(j, p, head, blocks, prepare=False):
                t = 2 * j + p
                if prepare:
                    dve.wait_ge(stats1_ready, t + 2)
                W = HALF * B
                if head == 0:
                    dve.wait_ge(q_t_ready, t + 1)
                for lb in blocks:
                    at = (head * LB + lb) * HD * HD * B
                    dve.wait_ge(conv_ready, 2 * LB * t + head * LB + lb + 1)
                    v.tensor_tensor(view(z, at, [[HALF, 2], [HD, W], [1, HALF]]),
                                    view(ps_y[lb], 0, [[PART, 2], [HALF, W], [1, HALF]]),
                                    view(q_t[p], lb * P + head * 2 * W, [[0, 2], [1, W], [0, HALF]]), ALU.mult)
                    v.tensor_tensor(view(z, at + HALF * HD * B, [[1, HD], [HD, B], [HD * B, HALF]]),
                                    view(ps_y[lb], PART, [[W, HD], [HALF, B], [1, HALF]]),
                                    view(q_t[p], lb * P + (head * 2 + 1) * W, [[0, HD], [1, B], [B, HALF]]),
                                    ALU.mult).then_inc(z_ready, 1)

            def sum_over_i(j, p, head, reuse, first=False):
                t = 2 * j + p
                n = 4 * t + 2 * head
                W = HD * B
                if first and head == 0:
                    dve.wait_ge(stats2_ready, t)
                dve.wait_ge(z_ready, 2 * LB * t + (head + 1) * LB)
                base = head * LB * HD * W
                v.tensor_tensor(view(z4, 0, [[4 * W, LB], [1, 4 * W]]),
                                view(z, base, [[HD * W, LB], [1, 4 * W]]),
                                view(z, base + 4 * W, [[HD * W, LB], [1, 4 * W]]), ALU.add).then_inc(sum_step, 1)
                dve.wait_ge(sum_step, n + 1)
                v.tensor_tensor(view(z2, 0, [[2 * W, LB], [1, 2 * W]]),
                                view(z4, 0, [[4 * W, LB], [1, 2 * W]]),
                                view(z4, 2 * W, [[4 * W, LB], [1, 2 * W]]), ALU.add).then_inc(sum_step, 1)
                dve.wait_ge(sum_step, n + 2)
                if head == 0 and reuse:
                    dve.wait_ge(attn_turned, t - 1)
                v.tensor_tensor(view(attn_t[p], head * W, [[P, LB], [1, B], [B, HD]]),
                                view(z2, 0, [[2 * W, LB], [HD, B], [1, HD]]),
                                view(z2, W, [[2 * W, LB], [HD, B], [1, HD]]), ALU.add).then_inc(attn_ready, 1)

            def residual_and_stats2(j, p, reuse):
                t = 2 * j + p
                dve.wait_ge(attn_turned, t + 1)
                dve.wait_ge(res_loaded[p], 16 * j + 16)
                if reuse:
                    dve.wait_ge(x1_b2_ready, t - 1)
                v.tensor_tensor(view(x1[p], 0, [[P, LB], [1, P]]), view(ps_t, P - 1, [[P, LB], [-1, P]]),
                                view(x_res[p], 0, [[P, LB], [1, P]]), ALU.add).then_inc(x1_ready, 1)
                dve.wait_ge(x1_ready, t + 1)
                v.bn_stats(stats2_buf[:], x1[p][:]).then_inc(stats2_ready, 1)

            def variance2(j, p, convolve):
                t = 2 * j + p
                if not convolve:
                    dve.wait_ge(stats2_ready, t + 1)
                v.bn_aggr(mv2[p][:], stats2_buf[:]).then_inc(mv2_step, 1)
                dve.wait_ge(mv2_step, 2 * t + 1)
                v.tensor_scalar(var2[p][:], mv2[p][:, 1:2], L * (1 + 1e-6), L * 1e-5 * 1e-6, ALU.mult, ALU.add
                                ).then_inc(var2_ready, 1)
                v.tensor_scalar(cent[:], x1[p][:], mv2[p][:, 0:1], None, ALU.subtract).then_inc(mv2_step, 1)
                dve.wait_ge(mv2_step, 2 * t + 2)
                v.tensor_reduce(cmax[p][:], cent[:], AX.X, ALU.max, apply_absolute_value=True
                                ).then_inc(cmax_ready, 1)

            def scales(t, largest, norm, mean_of, step, to_int, to_int_done, unit, unit_done):
                v.tensor_scalar(biggest[:, 0:1], largest[:], norm[:], 1e-5, ALU.mult, ALU.max).then_inc(step, 1)
                dve.wait_ge(step, 2 * t + 1)
                v.reciprocal(biggest[:, 1:2], biggest[:, 0:1]).then_inc(step, 1)
                dve.wait_ge(step, 2 * t + 2)
                v.tensor_scalar(to_int[:], biggest[:, 1:2], norm[:], 127.0, ALU.mult, ALU.mult
                                ).then_inc(to_int_done, 1)
                v.tensor_scalar(unit[:], biggest[:, 0:1], 1.0 / 127.0, mean_of, ALU.mult, ALU.mult
                                ).then_inc(unit_done, 1)

            def scale_tokens(j, p):
                t = 2 * j + p
                dve.wait_ge(cmax_ready, t + 1)
                dve.wait_ge(norm1_ready, t + 1)
                scales(t, cmax[p], norm1[p], w_mean[:, 0:1], scale1_step, to_int1[p], to_int1_ready,
                       unit1[p], unit1_ready)
                v.tensor_scalar(per_unit1[p][:, 0:1], biggest[:, 1:2], 127.0, w_mean_inv[:, 0:1],
                                ALU.mult, ALU.mult).then_inc(per_unit1_ready, 1)

            def quantise_tokens(j, p, others):
                t = 2 * j + p
                dve.wait_ge(to_int1_ready, t + 1)
                v.tensor_scalar(cent[:], cent[:], to_int1[p][:], MAGIC, ALU.mult, ALU.add).then_inc(xq_step, 1)
                dve.wait_ge(xq_step, t + 1)
                if others:
                    dve.wait_ge(xq_turned, t)
                v.tensor_scalar(xq[:, 0:L], cent[:], MAGIC, 127.0, ALU.subtract, ALU.min).then_inc(xq_ready, 1)

            def largest_g(j, p):
                t = 2 * j + p
                dve.wait_ge(g_ready, NCH * t + NCH)
                v.tensor_reduce(gmax[p][:], g[:], AX.X, ALU.max, apply_absolute_value=True
                                ).then_inc(gmax_ready, 1)

            def scale_g(j, p):
                t = 2 * j + p
                dve.wait_ge(gmax_ready, t + 1)
                dve.wait_ge(norm2_ready, t + 1)
                scales(t, gmax[p], norm2[p], w_mean[:, 1:2], scale2_step, to_int2[p], to_int2_ready,
                       unit2[p], unit2_ready)

            def quantise_g(j, p, others):
                t = 2 * j + p
                dve.wait_ge(g_rounded, t + 1)
                if others:
                    dve.wait_ge(gq_turned, 2 * t)
                v.tensor_scalar(gq[:], g[:], MAGIC, 127.0, ALU.subtract, ALU.min).then_inc(gq_ready, 1)

            def output(j, p, reuse):
                t = 2 * j + p
                dve.wait_ge(second_ready, t + 1)
                dve.wait_ge(x1_b2_ready, t + 1)
                dve.wait_ge(unit2_ready, t + 1)
                if reuse:
                    dve.wait_ge(stored[p], 16 * j)
                v.scalar_tensor_tensor(y_out[p][:], ps_f[p][:], unit2[p][:], x1_b2[p][:],
                                       ALU.mult, ALU.add).then_inc(y_ready, 1)

            stats1(0, 0)
            dve.wait_ge(stats1_ready, 1)
            variance1(0, 0)
            dve.wait_ge(kern_in, 32)
            dve.wait_ge(pads_set, 5)
            v.tensor_copy(kern_rev[:, 0:L], cent[0:H, L - 1::-1]).then_inc(kern_step, 1)
            dve.wait_ge(kern_step, 1)
            v.tensor_tensor(kern_rev[:, L - 1:L], kern_rev[:, L - 1:L], D_col[:], ALU.add).then_inc(kern_step, 1)
            dve.wait_ge(kern_step, 2)
            v.tensor_copy(kern_hi, kern_rev[:]).then_inc(kern_split, 1)
            dve.wait_ge(kern_split, 1)
            v.tensor_tensor(kern_lo, kern_rev[:], kern_hi.bitcast(F32), ALU.subtract).then_inc(kern_split, 1)
            b1v = b1_f32[0:3, :]
            dve.wait_ge(b1_in, 16)
            v.tensor_copy(b1_part[0][0:3, :], b1v).then_inc(b1_step, 1)
            dve.wait_ge(b1_step, 1)
            v.tensor_tensor(b1v, b1v, b1_part[0][0:3, :], ALU.subtract).then_inc(b1_step, 1)
            dve.wait_ge(b1_step, 2)
            v.tensor_copy(b1_part[1][0:3, :], b1v).then_inc(b1_step, 1)
            dve.wait_ge(b1_step, 3)
            v.tensor_tensor(b1v, b1v, b1_part[1][0:3, :], ALU.subtract).then_inc(b1_step, 1)
            dve.wait_ge(b1_step, 4)
            v.tensor_copy(b1_part[2][0:3, :], b1v).then_inc(b1_step, 1)
            make_q(0, 0)
            for m in range(2):
                with dve.Fori(0, 4) as j:
                    for s in range(4):
                        dve.wait_ge(w_in[s], 16 * j + 64 * m + 16)
                        v.tensor_reduce(abs_sums[:, m, bass.ds(4 * j + s, 1)], w_stage[s], AX.X, ALU.add,
                                        apply_absolute_value=True).then_inc(w_summed, 1)
                        dve.wait_ge(w_turned, 4 * j + 16 * m + s + 1)
                        src = w_bank[s].rearrange("p (k n) -> p k n", n=P)
                        if m == 0:
                            dst = w1s[:, :, bass.ds((4 * j + s) * P, P)]
                        else:
                            dst = w2s[:, 4 * s:4 * s + 4, bass.ds(j * P, P)]
                        v.tensor_copy(dst, src).then_inc(w_placed, 1)
            dve.wait_ge(w_summed, 32)
            v.tensor_reduce(abs_sum[:], abs_sums[:], AX.X, ALU.add).then_inc(w_total, 1)
            dve.wait_ge(w_total, 2)
            v.tensor_scalar(w_mean[:], ps_f[0][:, 0:2], 1.0 / (INNER * L), TINY, ALU.mult, ALU.max
                            ).then_inc(w_mean_step, 1)
            dve.wait_ge(w_mean_step, 1)
            v.reciprocal(w_mean_inv[:], w_mean[:]).then_inc(w_mean_ready, 1)
            dve.wait_ge(bias_in, 48)

            def iteration(j, p, prepare, convolve, first, second):
                now, one, two_, nxt = (before(j, p, n)[:2] for n in (0, 1, 2, -1))
                start = isinstance(j, int) and 2 * j + p <= 1
                if second:
                    largest_g(*two_)
                if prepare:
                    stats1(*nxt)
                if convolve:
                    multiply_q(*now, 0, range(0, 1), prepare)
                if prepare:
                    variance1(*nxt)
                if convolve:
                    multiply_q(*now, 0, range(1, 2))
                if second:
                    scale_g(*two_)
                if convolve:
                    multiply_q(*now, 0, range(2, LB))
                if first:
                    residual_and_stats2(*one, not (isinstance(j, int) and 2 * j + p <= 2))
                if convolve:
                    sum_over_i(*now, 0, not start, first)
                if first:
                    variance2(*one, convolve)
                if second:
                    quantise_g(*two_, not (isinstance(j, int) and 2 * j + p == 2))
                if prepare:
                    make_q(*nxt)
                if first:
                    scale_tokens(*one)
                if convolve:
                    multiply_q(*now, 1, range(0, 2))
                if first:
                    quantise_tokens(*one, second)
                if convolve:
                    multiply_q(*now, 1, range(2, LB))
                    sum_over_i(*now, 1, False)
                if second:
                    output(*two_, not (isinstance(j, int) and 2 * j + p <= 3))

            pipeline(dve, iteration)


_INS = ["x", "ctx_2048", "L0_xattn_ssm_kernel", "L0_xattn_D", "L0_ffn_w1", "L0_ffn_b1", "L0_ffn_w2", "L0_ffn_b2"]


def kernel(**inputs):
    import numpy as _np
    import concourse.bacc as _bacc
    from concourse.bass_utils import run_bass_kernel_spmd as _run

    nc = _bacc.Bacc("TRN2", target_bir_lowering=False, num_devices=1)
    arrays, args = {}, []
    for name in _INS:
        a = _np.ascontiguousarray(inputs[name])
        arrays[f"in_{name}"] = a
        args.append(nc.dram_tensor(f"in_{name}", a.shape, mybir.dt.from_np(a.dtype), kind="ExternalInput").ap())
    out = nc.dram_tensor("out", inputs["x"].shape, F32, kind="ExternalOutput").ap()
    build(nc, *args, out)
    return _run(nc, [arrays], core_ids=[0]).results[0]["out"]
```

```python
from contextlib import ExitStack

import concourse.bass as bass
from concourse import mybir

F32 = mybir.dt.float32
F32R = mybir.dt.float32r
BF16 = mybir.dt.bfloat16
ALU = mybir.AluOpType
ACT = mybir.ActivationFunctionType
AX = mybir.AxisListType

P = 128
MAGIC = 1.5 * 2.0**23
TINY = 1e-20


def view(tensor, offset, dims):
    whole = tensor[:]
    return bass.AP(tensor=whole.tensor, offset=whole.offset + offset,
                   ap=[list(whole.ap[0])] + [list(d) for d in dims])


def build(nc, x, ctx, ssm_kernel, D, w1, b1, w2, b2, out):
    B, CH, L = x.shape
    H = ssm_kernel.shape[0]
    HD = CH // H
    INNER = w1.shape[0]
    LB = L // P
    KB = INNER // P
    NCH = INNER // L
    HALF = HD // 2
    PART = HALF * B * HALF
    NPR = 3 * PART
    ROWS = 2 * HD
    TILES = CH // ROWS
    BAND = L + P
    assert ROWS * B == P and B == HD and L == 512 and TILES % 2 == 0 and NPR <= 512

    def rows_of(ap, t):
        return ap.rearrange("b (t r) d -> t r b d", r=ROWS)[bass.ds(t, 1)]

    kern_dram = nc.dram_tensor("kern_reversed", (2, H, BAND), F32, kind="Internal").ap()

    with ExitStack() as stack:
        def sb(name, shape, dt=F32):
            return stack.enter_context(nc.sbuf_tensor(name, shape, dt))

        def two(name, shape, dt=F32):
            return [sb(f"{name}{i}", shape, dt) for i in range(2)]

        def sem(name):
            return stack.enter_context(nc.semaphore(name))

        def sem2(name):
            return [sem(f"{name}{i}") for i in range(2)]

        ident = sb("ident", [P, P])
        ident_bf = sb("ident_bf", [P, P], BF16)
        ones = sb("ones", [P, P])
        magic = sb("magic", [P, 1])
        minus_half = sb("minus_half", [P, 1])
        inner_eps = sb("inner_eps", [P, 1])
        w1s = sb("w1s", [P, LB, INNER], BF16)
        w2s = sb("w2s", [P, KB, L], BF16)
        bias_rows = sb("bias_rows", [P, INNER], BF16)
        b2_all = sb("b2_all", [P, L])
        kern_rev = sb("kern_rev", [H, BAND])
        D_col = sb("D_col", [H, 1])
        abs_sums = sb("abs_sums", [P, 2, 8])
        abs_sum = sb("abs_sum", [P, 2])
        w_mean = sb("w_mean", [P, 2])
        w_mean_inv = sb("w_mean_inv", [P, 2])

        band = two("band", [P, 2, 2, L], F32R)
        x_in = two("x_in", [P, L])
        c_in = two("c_in", [P, L])
        x_res = two("x_res", [P, L])
        q_rev = sb("q_rev", [P, L])
        c_nat = sb("c_nat", [P, LB * P])
        c_bat = sb("c_bat", [P, LB * P])
        prod = sb("prod", [P, LB, 2, NPR])
        prod_hi = two("prod_hi", [P, LB, 2, NPR], F32R)
        prod_lo = two("prod_lo", [P, LB, 2, NPR], F32R)
        q_t = two("q_t", [P, LB, P])
        z = sb("z", [P, 2, LB, HD, HD * B])
        z4 = sb("z4", [P, LB, HD // 2, HD * B])
        z2 = sb("z2", [P, LB, HD // 4, HD * B])
        attn_t = two("attn_t", [P, LB, P])
        x1 = two("x1", [P, L])
        x1_b2 = two("x1_b2", [P, L])
        cent = sb("cent", [P, L])
        xq = sb("xq", [P, L + P], BF16)
        xq_t = sb("xq_t", [P, LB + 1, P], BF16)
        g = sb("g", [P, INNER])
        square_dump = sb("square_dump", [P, L], BF16)
        gq = sb("gq", [P, INNER], BF16)
        gq_t = sb("gq_t", [P, KB, P], BF16)
        y_out_both = sb("y_out", [P, 2, L])
        y_out = [y_out_both[:, i] for i in range(2)]
        stats1_buf = sb("stats1_buf", [P, nc.vector.BN_STATS_DIM])
        stats2_buf = sb("stats2_buf", [P, nc.vector.BN_STATS_DIM])
        mv1 = two("mv1", [P, 2])
        var1 = two("var1", [P, 1])
        rstd1 = two("rstd1", [P, 1])
        mv2 = two("mv2", [P, 2])
        cmax = two("cmax", [P, 1])
        var2 = two("var2", [P, 1])
        norm1 = two("norm1", [P, 1])
        norm2 = two("norm2", [P, 1])
        biggest = sb("biggest", [P, 2])
        to_int1 = two("to_int1", [P, 1])
        to_int2 = two("to_int2", [P, 1])
        unit1 = two("unit1", [P, 1])
        unit2 = two("unit2", [P, 1])
        per_unit1 = two("per_unit1", [P, 3])
        gsums = two("gsums", [P, NCH])
        gmaxs = two("gmaxs", [P, NCH])
        gsum = two("gsum", [P, 1])
        gmax = two("gmax", [P, 1])
        spare = prod_hi[1][0:H].rearrange("p a b c -> p (a b c)")
        kern_hi = spare[:, 0:BAND]
        kern_lo = spare[:, BAND:2 * BAND]
        w_stage = [y_out_both[:].rearrange("p a b -> p (a b)"),
                   gq_t[:].rearrange("p a b -> p (a b)").bitcast(F32)]
        w_sign = [gq[:, i * 2 * L:(i + 1) * 2 * L] for i in range(2)]
        w_dump = sb("w_dump", [P, 2 * L], BF16)
        b1_f32 = g
        b1_part = [z[:].rearrange("p a b c d -> p (a b c d)")[:, 2048:3072].bitcast(BF16),
                   z[:].rearrange("p a b c d -> p (a b c d)")[:, 3072:4096].bitcast(BF16),
                   z4[:].rearrange("p b c d -> p (b c d)")[:, 0:1024].bitcast(BF16)]

        ps_y = [stack.enter_context(nc.psum_tensor(f"ps_y{i}", [P, L], F32)) for i in range(LB)]
        ps_t = stack.enter_context(nc.psum_tensor("ps_t", [P, L], F32))
        ps_b = stack.enter_context(nc.psum_tensor("ps_b", [P, 2 * L], BF16))
        ps_f = [stack.enter_context(nc.psum_tensor(f"ps_f{i}", [P, L], F32)) for i in range(2)]

        w_bank = [bank[:].bitcast(BF16) for bank in ps_f]

        consts_set = sem("consts_set")
        pads_set = sem("pads_set")
        kern_in = sem("kern_in")
        kern_step = sem("kern_step")
        kern_split = sem("kern_split")
        kern_stored = sem("kern_stored")
        b1_in = sem("b1_in")
        b1_step = sem("b1_step")
        bias_in = sem("bias_in")
        b2_in = sem("b2_in")
        w_in = sem2("w_in")
        w_signed = sem("w_signed")
        w_summed = sem("w_summed")
        w_turned = sem("w_turned")
        w_placed = sem("w_placed")
        w_total = sem("w_total")
        w_totalled = sem("w_totalled")
        w_mean_step = sem("w_mean_step")
        w_mean_ready = sem("w_mean_ready")

        x_loaded = sem2("x_loaded")
        c_loaded = sem2("c_loaded")
        res_loaded = sem2("res_loaded")
        band_loaded = sem2("band_loaded")
        stored = sem2("stored")
        stats1_ready = sem("stats1_ready")
        mv1_step = sem("mv1_step")
        mv1_ready = sem("mv1_ready")
        rstd1_ready = sem("rstd1_ready")
        q_ready = sem("q_ready")
        q_turned = sem("q_turned")
        q_t_ready = sem("q_t_ready")
        c_turned = sem("c_turned")
        c_t_ready = sem("c_t_ready")
        prod_ready = sem("prod_ready")
        hi_ready = sem("hi_ready")
        lo_ready = sem("lo_ready")
        conv_ready = sem("conv_ready")
        z_ready = sem("z_ready")
        sum_step = sem("sum_step")
        attn_ready = sem("attn_ready")
        attn_turned = sem("attn_turned")
        x1_ready = sem("x1_ready")
        x1_b2_ready = sem("x1_b2_ready")
        stats2_ready = sem("stats2_ready")
        mv2_step = sem("mv2_step")
        cmax_ready = sem("cmax_ready")
        var2_ready = sem("var2_ready")
        norm1_ready = sem("norm1_ready")
        scale1_step = sem("scale1_step")
        to_int1_ready = sem("to_int1_ready")
        unit1_ready = sem("unit1_ready")
        per_unit1_ready = sem("per_unit1_ready")
        factor_step = sem("factor_step")
        factors_ready = sem("factors_ready")
        xq_step = sem("xq_step")
        xq_ready = sem("xq_ready")
        xq_turned = sem("xq_turned")
        xq_t_ready = sem("xq_t_ready")
        first_ready = sem("first_ready")
        g_ready = sem("g_ready")
        squares_ready = sem("squares_ready")
        gmaxs_ready = sem("gmaxs_ready")
        gsum_ready = sem("gsum_ready")
        gmax_ready = sem("gmax_ready")
        gsum_step = sem("gsum_step")
        norm2_ready = sem("norm2_ready")
        scale2_step = sem("scale2_step")
        to_int2_ready = sem("to_int2_ready")
        unit2_ready = sem("unit2_ready")
        g_rounded = sem("g_rounded")
        gq_ready = sem("gq_ready")
        gq_turned = sem("gq_turned")
        gq_t_ready = sem("gq_t_ready")
        second_ready = sem("second_ready")
        y_ready = sem("y_ready")

        block = stack.enter_context(nc.Block())

        def pipeline(eng, iteration):
            iteration(0, 0, True, True, False, False)
            iteration(0, 1, True, True, True, False)
            iteration(1, 0, True, True, True, True)
            iteration(1, 1, True, True, True, True)
            with eng.Fori(2, TILES // 2 - 1) as j:
                iteration(j, 0, True, True, True, True)
                iteration(j, 1, True, True, True, True)
            iteration(TILES // 2 - 1, 0, True, True, True, True)
            iteration(TILES // 2 - 1, 1, False, True, True, True)
            iteration(TILES // 2, 0, False, False, True, True)
            iteration(TILES // 2, 1, False, False, False, True)

        def before(j, p, n):
            pair, parity = j - (n - p + 1) // 2, (p - n) % 2
            return pair, parity, 2 * pair + parity

        @block.sync
        def _(sp):
            def load_x_and_c(j, p, waits=True):
                t = 2 * j + p
                if waits:
                    sp.wait_ge(q_ready, t - 1)
                sp.dma_start(x_in[p][:], rows_of(x, t)).then_inc(x_loaded[p], 16)
                if waits:
                    sp.wait_ge(c_turned, t - 1)
                sp.dma_start(c_in[p][:], rows_of(ctx, t)).then_inc(c_loaded[p], 16)

            def load_band(j, p, waits=True):
                t = 2 * j + p
                if waits:
                    sp.wait_ge(conv_ready, 2 * LB * (t - 1))
                for part in range(2):
                    whole = kern_dram[part]
                    src = bass.AP(tensor=whole.tensor, offset=whole.offset + 2 * BAND * t,
                                  ap=[[1, P], [BAND, 2], [1, L]])
                    sp.dma_start(band[p][:, part].bitcast(F32), src).then_inc(band_loaded[p], 16)

            def load_residual(j, p, waits=True):
                t = 2 * j + p
                if waits:
                    sp.wait_ge(x1_ready, t - 1)
                sp.dma_start(x_res[p][:], rows_of(x, t)).then_inc(res_loaded[p], 16)

            def store(j, p):
                sp.wait_ge(y_ready, 2 * j + p + 1)
                sp.dma_start(rows_of(out, 2 * j + p), y_out[p]).then_inc(stored[p], 16)

            w1_pairs = w1.rearrange("(k u p) n -> k p u n", u=2, p=P)
            w2_pairs = w2.rearrange("(r p) (k n) -> r k p n", p=P, n=2 * L)

            def load_weights(m, pairs):
                for k in pairs:
                    if m or k >= 2:
                        sp.wait_ge(w_signed, 8 * m + k - 1)
                        sp.wait_ge(w_summed, 8 * m + k - 1)
                    if m:
                        src, dst = w2_pairs[k // 2, k % 2], w_stage[k % 2]
                    else:
                        src, dst = w1_pairs[k], w_stage[k % 2].rearrange("p (u n) -> p u n", n=L)
                    sp.dma_start(dst, src).then_inc(w_in[k % 2], 16)

            load_x_and_c(0, 0, False)
            sp.dma_start(cent[0:H, :], ssm_kernel).then_inc(kern_in, 16)
            sp.dma_start(D_col[:], D.rearrange("(h a) -> h a", a=1)).then_inc(kern_in, 16)
            sp.dma_start(b1_f32[0:3, :], b1.rearrange("(a n) -> a n", a=1).to_broadcast([3, INNER])
                         ).then_inc(b1_in, 16)
            load_x_and_c(0, 1, False)
            sp.wait_ge(kern_split, 2)
            sp.dma_start(kern_dram[0], kern_hi.bitcast(F32)).then_inc(kern_stored, 16)
            sp.dma_start(kern_dram[1], kern_lo.bitcast(F32)).then_inc(kern_stored, 16)
            sp.dma_start(b2_all[:], b2.rearrange("(a n) -> a n", a=1).to_broadcast([P, L])
                         ).then_inc(b2_in, 16)

            sp.wait_ge(kern_stored, 32)
            load_band(0, 0, False)
            load_band(0, 1, False)
            load_residual(0, 0, False)
            load_residual(0, 1, False)
            load_weights(0, range(0, 2))
            sp.wait_ge(b1_step, 5)
            sp.wait_ge(pads_set, 5)
            for part in range(3):
                sp.dma_start(bias_rows[part:9:3, :], b1_part[part][0:3, :]).then_inc(bias_in, 16)

            def iteration(j, p, prepare, convolve, first, second):
                if prepare and not (isinstance(j, int) and 2 * j + p == TILES - 2):
                    load_x_and_c(j + 1, p)
                if first and convolve:
                    pair, parity, _ = before(j, p, -1)
                    if not (isinstance(j, int) and 2 * j + p == TILES - 1):
                        load_band(pair, parity)
                        load_residual(pair, parity)
                if second and not (isinstance(j, int) and 2 * j + p == 2):
                    pair, parity, _ = before(j, p, 3)
                    store(pair, parity)

            load_weights(0, range(2, 6))
            iteration(0, 0, True, True, False, False)
            load_weights(0, range(6, 8))
            load_weights(1, range(0, 4))
            iteration(0, 1, True, True, True, False)
            load_weights(1, range(4, 8))
            iteration(1, 0, True, True, True, True)
            iteration(1, 1, True, True, True, True)
            with sp.Fori(2, TILES // 2 - 1) as j:
                iteration(j, 0, True, True, True, True)
                iteration(j, 1, True, True, True, True)
            iteration(TILES // 2 - 1, 0, True, True, True, True)
            iteration(TILES // 2 - 1, 1, False, True, True, True)
            iteration(TILES // 2, 0, False, False, True, True)
            iteration(TILES // 2, 1, False, False, False, True)
            store(TILES // 2 - 1, 1)
            for p in range(2):
                sp.wait_ge(stored[p], 16 * TILES // 2)

        @block.tensor
        def _(pe):
            def turn_c(j, p):
                t = 2 * j + p
                pe.wait_ge(c_loaded[p], 16 * j + 16)
                pe.wait_ge(q_t_ready, t)
                for lb in range(LB):
                    last = nc.tensor.transpose(ps_t[:, lb * P:(lb + 1) * P],
                                               c_in[p][:, lb * P:(lb + 1) * P], ident[:])
                last.then_inc(c_turned, 1)

            def turn_q(j, p, others):
                t = 2 * j + p
                pe.wait_ge(q_ready, t + 1)
                pe.wait_ge(c_t_ready, 2 * t + 2)
                if others:
                    pe.wait_ge(x1_ready, t - 1)
                for lb in range(LB):
                    last = nc.tensor.transpose(ps_t[:, lb * P:(lb + 1) * P],
                                               q_rev[:, lb * P:(lb + 1) * P], ident[:])
                last.then_inc(q_turned, 1)

            def convolve_head(j, p, head, blocks=range(LB)):
                t = 2 * j + p
                if head == 0 and blocks[0] == 0:
                    pe.wait_ge(band_loaded[p], 32 * j + 32)
                for lb in blocks:
                    if head == 0 and lb % 2 == 0:
                        pe.wait_ge(hi_ready, 2 * t + lb // 2 + 1)
                        pe.wait_ge(lo_ready, 2 * t + lb // 2 + 1)
                    if head == 1 or not (isinstance(j, int) and t == 0):
                        pe.wait_ge(z_ready, 2 * LB * t + head * LB + lb - LB + 1)
                    n = 0
                    for mb in range(lb + 1):
                        at = (LB - 1 - (lb - mb)) * P
                        for kpart, ppart in ((0, 0), (0, 1), (1, 0)):
                            src = (prod_hi, prod_lo)[ppart][p]
                            last = nc.tensor.matmul(ps_y[lb][:, 0:NPR],
                                                    band[p][:, kpart, head, at:at + P],
                                                    src[:, mb, head, :],
                                                    start=(n == 0), stop=(n == 3 * lb + 2))
                            n += 1
                    last.then_inc(conv_ready, 1)

            def turn_attention(j, p, others):
                t = 2 * j + p
                pe.wait_ge(attn_ready, 2 * t + 2)
                if others:
                    pe.wait_ge(c_t_ready, 2 * t + 6)
                else:
                    pe.wait_ge(q_t_ready, t + 1)
                for lb in range(LB):
                    last = nc.tensor.transpose(ps_t[:, lb * P:(lb + 1) * P],
                                               attn_t[p][:, lb, :], ident[:])
                last.then_inc(attn_turned, 1)

            def turn_tokens(j, p, others):
                t = 2 * j + p
                pe.wait_ge(xq_ready, t + 1)
                pe.wait_ge(factors_ready, t + 1)
                if others:
                    pe.wait_ge(gq_t_ready, 2 * t)
                for kb in range(LB + 1):
                    last = nc.tensor.transpose(ps_b[:, kb * P:(kb + 1) * P],
                                               xq[:, kb * P:(kb + 1) * P], ident_bf[:])
                last.then_inc(xq_turned, 1)

            def first_product(j, p, others):
                t = 2 * j + p
                pe.wait_ge(xq_t_ready, t + 1)
                for n in range(NCH):
                    bank = ps_f[(p + n) % 2]
                    if n == 0 and others:
                        pe.wait_ge(g_ready, NCH * t)
                    if n == 1 and others:
                        pe.wait_ge(y_ready, t)
                    if n >= 2:
                        pe.wait_ge(g_ready, NCH * t + n - 1)
                    for kb in range(LB):
                        nc.tensor.matmul(bank[:], xq_t[:, kb, :], w1s[:, kb, n * L:(n + 1) * L],
                                         start=(kb == 0), stop=False)
                    nc.tensor.matmul(bank[:], xq_t[:, LB, :], bias_rows[:, n * L:(n + 1) * L],
                                     start=False, stop=True).then_inc(first_ready, 1)

            def turn_g(j, p, half):
                t = 2 * j + p
                pe.wait_ge(gq_ready, 2 * t + half + 1)
                if half == 0:
                    pe.wait_ge(xq_t_ready, t + 1)
                else:
                    pe.wait_ge(gq_t_ready, 2 * t + 1)
                for k in range(KB // 2):
                    kb = half * KB // 2 + k
                    last = nc.tensor.transpose(ps_b[:, k * P:(k + 1) * P],
                                               gq[:, kb * P:(kb + 1) * P], ident_bf[:])
                last.then_inc(gq_turned, 1)

            def second_product(j, p):
                t = 2 * j + p
                bank = ps_f[p]
                pe.wait_ge(gq_t_ready, 2 * t + 2)
                pe.wait_ge(g_ready, NCH * t + 3)
                for kb in range(KB):
                    last = nc.tensor.matmul(bank[:], gq_t[:, kb, :], w2s[:, kb, :],
                                            start=(kb == 0), stop=(kb == KB - 1))
                last.then_inc(second_ready, 1)

            pe.wait_ge(pads_set, 5)
            turn_c(0, 0)
            turn_q(0, 0, False)
            def turn_weights(m, pairs):
                for k in pairs:
                    pe.wait_ge(w_signed, 8 * m + k + 1)
                    if m or k >= 2:
                        pe.wait_ge(w_placed, 8 * m + k - 1)
                    if m and k < 2:
                        pe.wait_ge(w_mean_ready, 1)
                    for i in range(8):
                        last = nc.tensor.transpose(w_bank[k % 2][:, i * P:(i + 1) * P],
                                                   w_sign[k % 2][:, i * P:(i + 1) * P], ident_bf[:])
                    last.then_inc(w_turned, 1)

            def total_weights(m):
                pe.wait_ge(w_placed, 8 * m + 8)
                pe.wait_ge(w_total, m + 1)
                nc.tensor.matmul(ps_f[0][:, 0:2], ones[:], abs_sum[:], start=True, stop=True
                                 ).then_inc(w_totalled, 1)

            def iteration(j, p, prepare, convolve, first, second):
                now, one, two_, nxt = (before(j, p, n)[:2] for n in (0, 1, 2, -1))
                start = 2 * j + p if isinstance(j, int) else 99
                if prepare:
                    turn_c(*nxt)
                if start < 2:
                    turn_weights(start, range(0, 2))
                if convolve:
                    convolve_head(*now, 0, range(0, 3))
                if start < 2:
                    turn_weights(start, range(2, 4))
                if convolve:
                    convolve_head(*now, 0, range(3, LB))
                if first:
                    turn_attention(*one, prepare)
                if start < 2:
                    turn_weights(start, range(4, 6))
                if convolve:
                    convolve_head(*now, 1, range(0, 2))
                if second:
                    turn_g(*two_, 0)
                if convolve:
                    convolve_head(*now, 1, range(2, 3))
                if second:
                    turn_g(*two_, 1)
                if start < 2:
                    turn_weights(start, range(6, 8))
                if convolve:
                    convolve_head(*now, 1, range(3, LB))
                if second:
                    second_product(*two_)
                if start < 2:
                    total_weights(start)
                if first:
                    turn_tokens(*one, second)
                if prepare:
                    turn_q(*nxt, first)
                if start == 1:
                    pe.wait_ge(bias_in, 48)
                    pe.wait_ge(w_mean_ready, 2)
                if first:
                    first_product(*one, second)

            pipeline(pe, iteration)

        @block.scalar
        def _(act):
            def place_c(j, p):
                t = 2 * j + p
                act.wait_ge(c_turned, t + 1)
                act.wait_ge(prod_ready, 4 * t)
                nc.scalar.activation(c_nat[:], ps_t[:], ACT.Copy).then_inc(c_t_ready, 1)
                G = 4 * LB
                nc.scalar.activation(
                    c_bat[:].rearrange("m (g b i) -> m g b i", g=G, b=B),
                    ps_t[:].rearrange("m (g i b) -> m g b i", g=G, b=B), ACT.Copy).then_inc(c_t_ready, 1)

            def place_q(j, p, reuse):
                t = 2 * j + p
                act.wait_ge(q_turned, t + 1)
                if reuse:
                    act.wait_ge(z_ready, 2 * LB * (t - 1))
                nc.scalar.activation(q_t[p][:].rearrange("p a b -> p (a b)"), ps_t[:], ACT.Copy
                                     ).then_inc(q_t_ready, 1)

            def round_products(j, p, half, reuse):
                t = 2 * j + p
                act.wait_ge(prod_ready, 4 * t + 2 * half + 2)
                if half == 0 and reuse:
                    act.wait_ge(conv_ready, 2 * LB * (t - 1))
                nc.scalar.activation(prod_hi[p][:, 2 * half:2 * half + 2], prod[:, 2 * half:2 * half + 2],
                                     ACT.Copy).then_inc(hi_ready, 1)

            def bias_factors(j, p, others):
                t = 2 * j + p
                act.wait_ge(per_unit1_ready, t + 1)
                if others:
                    act.wait_ge(xq_turned, t)
                for part in range(3):
                    left = per_unit1[p][:, part:part + 1]
                    factor = xq[:, L + 3 * part:L + 3 * part + 3]
                    if part < 2:
                        nc.scalar.activation(factor, left.to_broadcast([P, 3]), ACT.Copy).then_inc(factor_step, 1)
                        act.wait_ge(factor_step, 4 * t + 2 * part + 1)
                        nc.scalar.activation(per_unit1[p][:, part + 1:part + 2], factor[:, 0:1], ACT.Identity,
                                             bias=left, scale=-1.0).then_inc(factor_step, 1)
                        act.wait_ge(factor_step, 4 * t + 2 * part + 2)
                    else:
                        nc.scalar.activation(factor, left.to_broadcast([P, 3]), ACT.Copy).then_inc(factors_ready, 1)

            def place_tokens(j, p, others):
                t = 2 * j + p
                act.wait_ge(xq_turned, t + 1)
                if others:
                    act.wait_ge(first_ready, NCH * t)
                nc.scalar.activation(xq_t[:].rearrange("p a b -> p (a b)"), ps_b[:, 0:(LB + 1) * P],
                                     ACT.Copy).then_inc(xq_t_ready, 1)

            def gelu(j, p, others):
                t = 2 * j + p
                if others:
                    act.wait_ge(gq_ready, 2 * t)
                act.wait_ge(unit1_ready, t + 1)
                for n in range(NCH):
                    act.wait_ge(first_ready, NCH * t + n + 1)
                    chunk = g[:, n * L:(n + 1) * L]
                    nc.scalar.activation(chunk, ps_f[(p + n) % 2][:], ACT.Gelu, scale=unit1[p][:]
                                         ).then_inc(g_ready, 1)
                    act.wait_ge(g_ready, NCH * t + n + 1)
                    nc.scalar.activation(square_dump[:], chunk, ACT.Square, accum_out=gsums[p][:, n:n + 1]
                                         ).then_inc(squares_ready, 1)

            def round_g(j, p, half):
                t = 2 * j + p
                if half == 0:
                    act.wait_ge(to_int2_ready, t + 1)
                part = g[:, half * INNER // 2:(half + 1) * INNER // 2]
                nc.scalar.activation(part, part, ACT.Identity, bias=magic[:], scale=to_int2[p][:]
                                     ).then_inc(g_rounded, 1)

            def place_g(j, p, half, others):
                t = 2 * j + p
                act.wait_ge(gq_turned, 2 * t + half + 1)
                if half == 0 and others:
                    act.wait_ge(second_ready, t)
                nc.scalar.activation(gq_t[:, half * KB // 2:(half + 1) * KB // 2, :].rearrange("p a b -> p (a b)"),
                                     ps_b[:], ACT.Copy).then_inc(gq_t_ready, 1)

            place_c(0, 0)
            place_q(0, 0, False)
            for half in range(2):
                round_products(0, 0, half, False)
            act.wait_ge(kern_stored, 32)

            def sign_weights(m, pairs):
                for k in pairs:
                    act.wait_ge(w_in[k % 2], 64 * m + 16 * (k // 2) + 16)
                    if m or k >= 2:
                        act.wait_ge(w_turned, 8 * m + k - 1)
                    nc.scalar.activation(w_sign[k % 2], w_stage[k % 2], ACT.Sign).then_inc(w_signed, 1)
                    if m or k:
                        act.wait_ge(w_summed, 8 * m + k)
                    nc.scalar.activation(w_dump[:], w_stage[k % 2], ACT.Abs, accum_out=abs_sums[:, m, k:k + 1]
                                         ).then_inc(w_summed, 1)

            def iteration(j, p, prepare, convolve, first, second):
                now, one, two_, nxt = (before(j, p, n)[:2] for n in (0, 1, 2, -1))
                start = 2 * j + p if isinstance(j, int) else 99
                if prepare:
                    place_c(*nxt)
                if start < 2:
                    sign_weights(start, range(0, 4))
                if second:
                    round_g(*two_, 0)
                    round_g(*two_, 1)
                if prepare:
                    round_products(*nxt, 0, first)
                if start < 2:
                    sign_weights(start, range(4, 6))
                if second:
                    place_g(*two_, 0, start != 2)
                if prepare:
                    round_products(*nxt, 1, first)
                if start < 2:
                    sign_weights(start, range(6, 8))
                if second:
                    place_g(*two_, 1, True)
                if first:
                    bias_factors(*one, second)
                    place_tokens(*one, second)
                if prepare:
                    place_q(*nxt, first)
                if first:
                    gelu(*one, second)

            pipeline(act, iteration)

        @block.gpsimd
        def _(pool):
            pe_ = nc.gpsimd

            def make_rstd1(j, p):
                t = 2 * j + p
                pool.wait_ge(mv1_ready, t + 1)
                pe_.tensor_tensor(rstd1[p][:], var1[p][:], minus_half[:], ALU.pow).then_inc(rstd1_ready, 1)

            def multiply_c(j, p, half):
                t = 2 * j + p
                if half == 0:
                    pool.wait_ge(c_t_ready, 2 * t + 2)
                    pool.wait_ge(hi_ready, 2 * t)
                    pool.wait_ge(lo_ready, 2 * t)
                W = HALF * B
                for part, heads, o1, o2, step, count in ((0, 2, 0, 0, 2 * PART, 2), (1, 1, 0, W, 0, 1)):
                    n = 4 * heads
                    base = half * 2 * P
                    left = view(c_nat, base + o1, [[2 * W // heads, n], [1, W], [0, HALF]])
                    right = view(c_bat, base + o2, [[2 * W // heads, n], [0, HALF], [1, W]])
                    if part == 0:
                        dst = view(prod, half * 4 * NPR, [[NPR, 4], [2 * PART, 2], [1, PART]])
                    else:
                        dst = view(prod, half * 4 * NPR + PART, [[NPR, 4], [1, PART]])
                    pe_.tensor_tensor(dst, left, right, ALU.mult).then_inc(prod_ready, 1)

            def remainders(j, p, half):
                t = 2 * j + p
                pool.wait_ge(hi_ready, 2 * t + half + 1)
                hi = prod_hi[p][:, 2 * half:2 * half + 2].bitcast(F32)
                pe_.tensor_tensor(prod_lo[p][:, 2 * half:2 * half + 2], prod[:, 2 * half:2 * half + 2], hi,
                                  ALU.subtract).then_inc(lo_ready, 1)

            def make_norm1(j, p):
                t = 2 * j + p
                pool.wait_ge(var2_ready, t + 1)
                pe_.tensor_tensor(norm1[p][:], var2[p][:], minus_half[:], ALU.pow).then_inc(norm1_ready, 1)

            def add_b2(j, p, reuse):
                t = 2 * j + p
                pool.wait_ge(x1_ready, t + 1)
                if reuse:
                    pool.wait_ge(y_ready, t - 1)
                pe_.tensor_tensor(x1_b2[p][:], x1[p][:], b2_all[:], ALU.add).then_inc(x1_b2_ready, 1)

            def make_norm2(j, p):
                t = 2 * j + p
                pool.wait_ge(gsum_ready, t + 1)
                pe_.tensor_tensor(gsum[p][:], gsum[p][:], inner_eps[:], ALU.add).then_inc(gsum_step, 1)
                pool.wait_ge(gsum_step, t + 1)
                pe_.tensor_tensor(norm2[p][:], gsum[p][:], minus_half[:], ALU.pow).then_inc(norm2_ready, 1)

            for m, value in ((ident, 0.0), (ones, 1.0), (magic, MAGIC), (minus_half, -0.5),
                             (inner_eps, INNER * 1e-6)):
                pe_.memset(m[:], value).then_inc(consts_set, 1)
            pool.wait_ge(consts_set, 5)
            pe_.affine_select(out=ident[:], in_=ident[:], compare_op=ALU.not_equal, fill=1.0, base=0,
                              pattern=[[-1, P]], channel_multiplier=1).then_inc(pads_set, 1)
            pool.wait_ge(pads_set, 1)
            pe_.tensor_copy(ident_bf[:], ident[:]).then_inc(pads_set, 1)
            pe_.memset(kern_rev[:, L:BAND], 0.0).then_inc(pads_set, 1)
            pe_.memset(bias_rows[:], 0.0).then_inc(pads_set, 1)
            pe_.memset(xq[:], 0.0).then_inc(pads_set, 1)
            make_rstd1(0, 0)
            multiply_c(0, 0, 0)
            multiply_c(0, 0, 1)
            remainders(0, 0, 0)
            remainders(0, 0, 1)
            pool.wait_ge(b2_in, 16)

            def iteration(j, p, prepare, convolve, first, second):
                now, one, two_, nxt = (before(j, p, n)[:2] for n in (0, 1, 2, -1))
                if second:
                    make_norm2(*two_)
                if prepare:
                    make_rstd1(*nxt)
                    multiply_c(*nxt, 0)
                    multiply_c(*nxt, 1)
                if first:
                    make_norm1(*one)
                if prepare:
                    remainders(*nxt, 0)
                if first:
                    add_b2(*one, not (isinstance(j, int) and 2 * j + p <= 2))
                if prepare:
                    remainders(*nxt, 1)

            pipeline(pool, iteration)

        @block.vector
        def _(dve):
            v = nc.vector

            def stats1(j, p):
                dve.wait_ge(x_loaded[p], 16 * j + 16)
                v.bn_stats(stats1_buf[:], x_in[p][:]).then_inc(stats1_ready, 1)

            def variance1(j, p):
                t = 2 * j + p
                v.bn_aggr(mv1[p][:], stats1_buf[:]).then_inc(mv1_step, 1)
                dve.wait_ge(mv1_step, t + 1)
                v.tensor_scalar(var1[p][:], mv1[p][:, 1:2], 1e-5, None, ALU.add).then_inc(mv1_ready, 1)

            def make_q(j, p):
                t = 2 * j + p
                dve.wait_ge(rstd1_ready, t + 1)
                dve.wait_ge(q_turned, t)
                v.tensor_scalar(view(q_rev, 0, [[P, LB], [1, P]]), view(x_in[p], P - 1, [[P, LB], [-1, P]]),
                                mv1[p][:, 0:1], rstd1[p][:], ALU.subtract, ALU.mult).then_inc(q_ready, 1)

            def multiply_q(j, p, head, blocks, prepare=False):
                t = 2 * j + p
                if prepare:
                    dve.wait_ge(stats1_ready, t + 2)
                W = HALF * B
                if head == 0:
                    dve.wait_ge(q_t_ready, t + 1)
                for lb in blocks:
                    at = (head * LB + lb) * HD * HD * B
                    dve.wait_ge(conv_ready, 2 * LB * t + head * LB + lb + 1)
                    v.tensor_tensor(view(z, at, [[HALF, 2], [HD, W], [1, HALF]]),
                                    view(ps_y[lb], 0, [[PART, 2], [HALF, W], [1, HALF]]),
                                    view(q_t[p], lb * P + head * 2 * W, [[0, 2], [1, W], [0, HALF]]), ALU.mult)
                    v.tensor_tensor(view(z, at + HALF * HD * B, [[1, HD], [HD, B], [HD * B, HALF]]),
                                    view(ps_y[lb], PART, [[W, HD], [HALF, B], [1, HALF]]),
                                    view(q_t[p], lb * P + (head * 2 + 1) * W, [[0, HD], [1, B], [B, HALF]]),
                                    ALU.mult).then_inc(z_ready, 1)

            def sum_over_i(j, p, head, reuse):
                t = 2 * j + p
                n = 4 * t + 2 * head
                W = HD * B
                dve.wait_ge(z_ready, 2 * LB * t + (head + 1) * LB)
                base = head * LB * HD * W
                v.tensor_tensor(view(z4, 0, [[4 * W, LB], [1, 4 * W]]),
                                view(z, base, [[HD * W, LB], [1, 4 * W]]),
                                view(z, base + 4 * W, [[HD * W, LB], [1, 4 * W]]), ALU.add).then_inc(sum_step, 1)
                dve.wait_ge(sum_step, n + 1)
                v.tensor_tensor(view(z2, 0, [[2 * W, LB], [1, 2 * W]]),
                                view(z4, 0, [[4 * W, LB], [1, 2 * W]]),
                                view(z4, 2 * W, [[4 * W, LB], [1, 2 * W]]), ALU.add).then_inc(sum_step, 1)
                dve.wait_ge(sum_step, n + 2)
                if head == 0 and reuse:
                    dve.wait_ge(attn_turned, t - 1)
                v.tensor_tensor(view(attn_t[p], head * W, [[P, LB], [1, B], [B, HD]]),
                                view(z2, 0, [[2 * W, LB], [HD, B], [1, HD]]),
                                view(z2, W, [[2 * W, LB], [HD, B], [1, HD]]), ALU.add).then_inc(attn_ready, 1)

            def residual_and_stats2(j, p, reuse):
                t = 2 * j + p
                dve.wait_ge(attn_turned, t + 1)
                dve.wait_ge(res_loaded[p], 16 * j + 16)
                if reuse:
                    dve.wait_ge(x1_b2_ready, t - 1)
                v.tensor_tensor(view(x1[p], 0, [[P, LB], [1, P]]), view(ps_t, P - 1, [[P, LB], [-1, P]]),
                                view(x_res[p], 0, [[P, LB], [1, P]]), ALU.add).then_inc(x1_ready, 1)
                dve.wait_ge(x1_ready, t + 1)
                v.bn_stats(stats2_buf[:], x1[p][:]).then_inc(stats2_ready, 1)

            def variance2(j, p):
                t = 2 * j + p
                if isinstance(j, int):
                    dve.wait_ge(stats2_ready, t + 1)
                v.bn_aggr(mv2[p][:], stats2_buf[:]).then_inc(mv2_step, 1)
                dve.wait_ge(mv2_step, 2 * t + 1)
                v.tensor_scalar(var2[p][:], mv2[p][:, 1:2], L * (1 + 1e-6), L * 1e-5 * 1e-6, ALU.mult, ALU.add
                                ).then_inc(var2_ready, 1)
                v.tensor_scalar(cent[:], x1[p][:], mv2[p][:, 0:1], None, ALU.subtract).then_inc(mv2_step, 1)
                dve.wait_ge(mv2_step, 2 * t + 2)
                v.tensor_reduce(cmax[p][:], cent[:], AX.X, ALU.max, apply_absolute_value=True
                                ).then_inc(cmax_ready, 1)

            def scales(t, largest, norm, mean_of, step, to_int, to_int_done, unit, unit_done):
                v.tensor_scalar(biggest[:, 0:1], largest[:], norm[:], 1e-5, ALU.mult, ALU.max).then_inc(step, 1)
                dve.wait_ge(step, 2 * t + 1)
                v.reciprocal(biggest[:, 1:2], biggest[:, 0:1]).then_inc(step, 1)
                dve.wait_ge(step, 2 * t + 2)
                v.tensor_scalar(to_int[:], biggest[:, 1:2], norm[:], 127.0, ALU.mult, ALU.mult
                                ).then_inc(to_int_done, 1)
                v.tensor_scalar(unit[:], biggest[:, 0:1], 1.0 / 127.0, mean_of, ALU.mult, ALU.mult
                                ).then_inc(unit_done, 1)

            def scale_tokens(j, p):
                t = 2 * j + p
                dve.wait_ge(cmax_ready, t + 1)
                dve.wait_ge(norm1_ready, t + 1)
                scales(t, cmax[p], norm1[p], w_mean[:, 0:1], scale1_step, to_int1[p], to_int1_ready,
                       unit1[p], unit1_ready)
                v.tensor_scalar(per_unit1[p][:, 0:1], biggest[:, 1:2], 127.0, w_mean_inv[:, 0:1],
                                ALU.mult, ALU.mult).then_inc(per_unit1_ready, 1)

            def quantise_tokens(j, p, others):
                t = 2 * j + p
                dve.wait_ge(to_int1_ready, t + 1)
                v.tensor_scalar(cent[:], cent[:], to_int1[p][:], MAGIC, ALU.mult, ALU.add).then_inc(xq_step, 1)
                dve.wait_ge(xq_step, t + 1)
                if others:
                    dve.wait_ge(xq_turned, t)
                v.tensor_scalar(xq[:, 0:L], cent[:], MAGIC, 127.0, ALU.subtract, ALU.min).then_inc(xq_ready, 1)

            def largest_g(j, p, chunks):
                t = 2 * j + p
                for n in chunks:
                    dve.wait_ge(g_ready, NCH * t + n + 1)
                    v.tensor_reduce(gmaxs[p][:, n:n + 1], g[:, n * L:(n + 1) * L], AX.X, ALU.max,
                                    apply_absolute_value=True).then_inc(gmaxs_ready, 1)

            def combine_g(j, p):
                t = 2 * j + p
                dve.wait_ge(gmaxs_ready, NCH * t + NCH)
                v.tensor_reduce(gmax[p][:], gmaxs[p][:], AX.X, ALU.max).then_inc(gmax_ready, 1)
                dve.wait_ge(squares_ready, NCH * t + NCH)
                v.tensor_reduce(gsum[p][:], gsums[p][:], AX.X, ALU.add).then_inc(gsum_ready, 1)

            def scale_g(j, p):
                t = 2 * j + p
                dve.wait_ge(gmax_ready, t + 1)
                dve.wait_ge(norm2_ready, t + 1)
                scales(t, gmax[p], norm2[p], w_mean[:, 1:2], scale2_step, to_int2[p], to_int2_ready,
                       unit2[p], unit2_ready)

            def quantise_g(j, p, half, others, first=False):
                t = 2 * j + p
                if first:
                    dve.wait_ge(stats2_ready, t + 2)
                dve.wait_ge(g_rounded, 2 * t + half + 1)
                if others and half == 0:
                    dve.wait_ge(gq_turned, 2 * t)
                at = slice(half * INNER // 2, (half + 1) * INNER // 2)
                v.tensor_scalar(gq[:, at], g[:, at], MAGIC, 127.0, ALU.subtract, ALU.min).then_inc(gq_ready, 1)

            def output(j, p, reuse):
                t = 2 * j + p
                dve.wait_ge(second_ready, t + 1)
                dve.wait_ge(x1_b2_ready, t + 1)
                dve.wait_ge(unit2_ready, t + 1)
                if reuse:
                    dve.wait_ge(stored[p], 16 * j)
                v.scalar_tensor_tensor(y_out[p], ps_f[p][:], unit2[p][:], x1_b2[p][:],
                                       ALU.mult, ALU.add).then_inc(y_ready, 1)

            stats1(0, 0)
            dve.wait_ge(stats1_ready, 1)
            variance1(0, 0)
            dve.wait_ge(kern_in, 32)
            dve.wait_ge(pads_set, 5)
            v.tensor_copy(kern_rev[:, 0:L], cent[0:H, L - 1::-1]).then_inc(kern_step, 1)
            dve.wait_ge(kern_step, 1)
            v.tensor_tensor(kern_rev[:, L - 1:L], kern_rev[:, L - 1:L], D_col[:], ALU.add).then_inc(kern_step, 1)
            dve.wait_ge(kern_step, 2)
            v.tensor_copy(kern_hi, kern_rev[:]).then_inc(kern_split, 1)
            dve.wait_ge(kern_split, 1)
            v.tensor_tensor(kern_lo, kern_rev[:], kern_hi.bitcast(F32), ALU.subtract).then_inc(kern_split, 1)
            b1v = b1_f32[0:3, :]
            dve.wait_ge(b1_in, 16)
            v.tensor_copy(b1_part[0][0:3, :], b1v).then_inc(b1_step, 1)
            dve.wait_ge(b1_step, 1)
            v.tensor_tensor(b1v, b1v, b1_part[0][0:3, :], ALU.subtract).then_inc(b1_step, 1)
            dve.wait_ge(b1_step, 2)
            v.tensor_copy(b1_part[1][0:3, :], b1v).then_inc(b1_step, 1)
            dve.wait_ge(b1_step, 3)
            v.tensor_tensor(b1v, b1v, b1_part[1][0:3, :], ALU.subtract).then_inc(b1_step, 1)
            dve.wait_ge(b1_step, 4)
            v.tensor_copy(b1_part[2][0:3, :], b1v).then_inc(b1_step, 1)
            make_q(0, 0)
            dve.wait_ge(bias_in, 48)

            def place_weights(m, pairs):
                for k in pairs:
                    dve.wait_ge(w_turned, 8 * m + k + 1)
                    src = w_bank[k % 2]
                    if m:
                        at = k % 2 * 8
                        dst = w2s[:, at:at + 8, k // 2 * P:(k // 2 + 1) * P]
                        v.tensor_copy(dst, src.rearrange("p (c n) -> p c n", n=P)).then_inc(w_placed, 1)
                    else:
                        v.tensor_copy(view(w1s, 2 * k * P, [[P, 2], [INNER, LB], [1, P]]),
                                      src.rearrange("p (u c n) -> p u c n", u=2, n=P)).then_inc(w_placed, 1)

            def mean_of_weights(m):
                dve.wait_ge(w_summed, 8 * m + 8)
                if m == 0:
                    v.memset(abs_sum[:, 1:2], 0.0).then_inc(w_mean_step, 1)
                v.tensor_reduce(abs_sum[:, m:m + 1], abs_sums[:, m], AX.X, ALU.add).then_inc(w_total, 1)
                dve.wait_ge(w_totalled, m + 1)
                v.tensor_scalar(w_mean[:, m:m + 1], ps_f[0][:, m:m + 1], 1.0 / (INNER * L), TINY,
                                ALU.mult, ALU.max).then_inc(w_mean_step, 1)
                dve.wait_ge(w_mean_step, m + 2)
                v.reciprocal(w_mean_inv[:, m:m + 1], w_mean[:, m:m + 1]).then_inc(w_mean_ready, 1)

            def iteration(j, p, prepare, convolve, first, second):
                now, one, two_, nxt = (before(j, p, n)[:2] for n in (0, 1, 2, -1))
                start = 2 * j + p if isinstance(j, int) else 99
                if second:
                    largest_g(*two_, range(3, NCH))
                if prepare:
                    stats1(*nxt)
                if second:
                    combine_g(*two_)
                if start < 2:
                    place_weights(start, range(0, 2))
                if convolve:
                    multiply_q(*now, 0, range(0, 1), prepare)
                if prepare:
                    variance1(*nxt)
                if convolve:
                    multiply_q(*now, 0, range(1, 2))
                if second:
                    scale_g(*two_)
                if convolve:
                    multiply_q(*now, 0, range(2, 3))
                if start < 2:
                    place_weights(start, range(2, 4))
                if second:
                    quantise_g(*two_, 0, start != 2)
                if prepare:
                    make_q(*nxt)
                if convolve:
                    multiply_q(*now, 0, range(3, LB))
                if first:
                    residual_and_stats2(*one, start > 2)
                if start < 2:
                    place_weights(start, range(4, 6))
                if second:
                    quantise_g(*two_, 1, True, first)
                if first:
                    variance2(*one)
                if convolve:
                    multiply_q(*now, 1, range(0, 2))
                if first:
                    scale_tokens(*one)
                    quantise_tokens(*one, second)
                if convolve:
                    multiply_q(*now, 1, range(2, 3))
                    sum_over_i(*now, 0, start > 1)
                if start < 2:
                    place_weights(start, range(6, 8))
                if convolve:
                    multiply_q(*now, 1, range(3, LB))
                if start < 2:
                    mean_of_weights(start)
                if second:
                    output(*two_, start > 3)
                if convolve:
                    sum_over_i(*now, 1, False)
                if first:
                    largest_g(*one, range(0, 3))

            pipeline(dve, iteration)


_INS = ["x", "ctx_2048", "L0_xattn_ssm_kernel", "L0_xattn_D", "L0_ffn_w1", "L0_ffn_b1", "L0_ffn_w2", "L0_ffn_b2"]


def kernel(**inputs):
    import numpy as _np
    import concourse.bacc as _bacc
    from concourse.bass_utils import run_bass_kernel_spmd as _run

    nc = _bacc.Bacc("TRN2", target_bir_lowering=False, num_devices=1)
    arrays, args = {}, []
    for name in _INS:
        a = _np.ascontiguousarray(inputs[name])
        arrays[f"in_{name}"] = a
        args.append(nc.dram_tensor(f"in_{name}", a.shape, mybir.dt.from_np(a.dtype), kind="ExternalInput").ap())
    out = nc.dram_tensor("out", inputs["x"].shape, F32, kind="ExternalOutput").ap()
    build(nc, *args, out)
    return _run(nc, [arrays], core_ids=[0]).results[0]["out"]
```

```python
from contextlib import ExitStack

import concourse.bass as bass
from concourse import mybir

F32 = mybir.dt.float32
F32R = mybir.dt.float32r
BF16 = mybir.dt.bfloat16
ALU = mybir.AluOpType
ACT = mybir.ActivationFunctionType
AX = mybir.AxisListType

P = 128
MAGIC = 1.5 * 2.0**23
TINY = 1e-20


def view(tensor, offset, dims):
    whole = tensor[:]
    return bass.AP(tensor=whole.tensor, offset=whole.offset + offset,
                   ap=[list(whole.ap[0])] + [list(d) for d in dims])


def build(nc, x, ctx, ssm_kernel, D, w1, b1, w2, b2, out):
    B, CH, L = x.shape
    H = ssm_kernel.shape[0]
    HD = CH // H
    INNER = w1.shape[0]
    LB = L // P
    KB = INNER // P
    NCH = INNER // L
    HALF = HD // 2
    CH8 = HD * B
    EXT = CH8 + HALF * B
    NPR = (HALF + 1) * CH8
    ROW = CH8 + (HALF - 1) * B
    ZS = HALF * CH8 + HALF * ROW
    FOLD = 2 * CH8 + 2 * ROW
    ROWS = 2 * HD
    TILES = CH // ROWS
    BAND = L + P
    assert ROWS * B == P and B == HD and L == 512 and TILES % 2 == 0 and NPR <= 512

    def rows_of(ap, t):
        return ap.rearrange("b (t r) d -> t r b d", r=ROWS)[bass.ds(t, 1)]

    kern_dram = nc.dram_tensor("kern_reversed", (2, H, BAND), F32, kind="Internal").ap()
    b1_dram = nc.dram_tensor("b1_parts", (3, INNER), BF16, kind="Internal").ap()

    with ExitStack() as stack:
        def sb(name, shape, dt=F32):
            return stack.enter_context(nc.sbuf_tensor(name, shape, dt))

        def two(name, shape, dt=F32):
            return [sb(f"{name}{i}", shape, dt) for i in range(2)]

        def sem(name):
            return stack.enter_context(nc.semaphore(name))

        def sem2(name):
            return [sem(f"{name}{i}") for i in range(2)]

        ident = sb("ident", [P, P])
        ident_bf = sb("ident_bf", [P, P], BF16)
        ones = sb("ones", [P, P])
        magic = sb("magic", [P, 1])
        gelu_first = sb("gelu_first", [P, 1])
        minus_half = sb("minus_half", [P, 1])
        inner_eps = sb("inner_eps", [P, 1])
        w1s = sb("w1s", [P, LB, INNER], BF16)
        w2s = sb("w2s", [P, KB, L], BF16)
        bias_rows = sb("bias_rows", [P, INNER], BF16)
        b2_all = sb("b2_all", [P, L])
        kern_rev = sb("kern_rev", [H, BAND])
        D_col = sb("D_col", [H, 1])
        abs_sums = sb("abs_sums", [P, 2, 8])
        abs_sum = sb("abs_sum", [P, 2])
        w_mean = sb("w_mean", [P, 2])
        w_mean_inv = sb("w_mean_inv", [P, 2])

        band = two("band", [P, 2, 2, L], F32R)
        x_in = two("x_in", [P, L])
        c_in = two("c_in", [P, L])
        x_res = two("x_res", [P, L])
        q_rev = sb("q_rev", [P, L])
        c_ext = sb("c_ext", [P, LB * 2 * EXT])
        prod = sb("prod", [P, LB, 2, NPR])
        prod_hi = two("prod_hi", [P, LB, 2, NPR], F32R)
        prod_lo = two("prod_lo", [P, LB, 2, NPR], F32R)
        q_ext = two("q_ext", [P, LB * 2 * EXT])
        z = sb("z", [P, 2 * LB * ZS])
        folded = [sb(f"folded_head{i}", [P, LB * FOLD]) for i in range(2)]
        attn_t = two("attn_t", [P, LB, P])
        x1 = two("x1", [P, L])
        x1_b2 = two("x1_b2", [P, L])
        cent = sb("cent", [P, L])
        xq = sb("xq", [P, L + P], BF16)
        xq_t = sb("xq_t", [P, LB + 1, P], BF16)
        g = sb("g", [P, INNER])
        gq = sb("gq", [P, INNER], BF16)
        gq_t = sb("gq_t", [P, KB, P], BF16)
        y_out_both = sb("y_out", [P, 2, L])
        y_out = [y_out_both[:, i] for i in range(2)]
        stats1_buf = sb("stats1_buf", [P, nc.vector.BN_STATS_DIM])
        stats2_buf = sb("stats2_buf", [P, nc.vector.BN_STATS_DIM])
        mv1 = two("mv1", [P, 2])
        var1 = two("var1", [P, 1])
        rstd1 = two("rstd1", [P, 1])
        mv2 = two("mv2", [P, 2])
        neg_mean2 = two("neg_mean2", [P, 1])
        cmax = two("cmax", [P, 1])
        var2 = two("var2", [P, 1])
        norm1 = two("norm1", [P, 1])
        norm2 = two("norm2", [P, 1])
        biggest = sb("biggest", [P, 2])
        to_int1 = two("to_int1", [P, 1])
        to_int2 = two("to_int2", [P, 1])
        unit1 = two("unit1", [P, 1])
        unit2 = two("unit2", [P, 1])
        per_unit1 = two("per_unit1", [P, 3])
        gsums = two("gsums", [P, NCH])
        gmaxs = two("gmaxs", [P, NCH])
        gsum = two("gsum", [P, 1])
        gmax = two("gmax", [P, 1])
        spare = prod_hi[1][0:H].rearrange("p a b c -> p (a b c)")
        kern_hi = spare[:, 0:BAND]
        kern_lo = spare[:, BAND:2 * BAND]
        w_stage = [y_out_both[:].rearrange("p a b -> p (a b)"),
                   gq_t[:].rearrange("p a b -> p (a b)").bitcast(F32),
                   g[:, 0:2 * L], g[:, 2 * L:4 * L]]
        STAGES = len(w_stage)
        W_PAIRS = INNER // (2 * P)
        w_sign = [gq[:, 0:2 * L], gq[:, 2 * L:4 * L], x1[1][:].bitcast(BF16), x1_b2[1][:].bitcast(BF16)]
        SIGNS = len(w_sign)
        w_dump = sb("w_dump", [P, 2 * L], BF16)
        square_dump = w_dump[:].rearrange("p (a n) -> p a n", a=2)
        b1_cols = sb("b1_cols", [P, INNER // P])
        b1_parts = sb("b1_parts_sb", [P, 3, INNER // P], BF16)

        ps_y = [stack.enter_context(nc.psum_tensor(f"ps_y{i}", [P, L], F32)) for i in range(LB)]
        ps_t = stack.enter_context(nc.psum_tensor("ps_t", [P, L], F32))
        ps_b = stack.enter_context(nc.psum_tensor("ps_b", [P, 2 * L], BF16))
        ps_f = [stack.enter_context(nc.psum_tensor(f"ps_f{i}", [P, L], F32)) for i in range(2)]

        w_bank = [ps_f[0][:].bitcast(BF16), ps_f[1][:].bitcast(BF16), ps_b[:]]
        W_BANKS = len(w_bank)
        g_last = z[:, 0:INNER]
        ps_b2 = ps_t[:].bitcast(BF16)

        consts_set = sem("consts_set")
        pads_set = sem("pads_set")
        kern_in = sem("kern_in")
        kern_step = sem("kern_step")
        kern_split = sem("kern_split")
        kern_stored = sem("kern_stored")
        b1_in = sem("b1_in")
        b1_step = sem("b1_step")
        b1_stored = sem("b1_stored")
        bias_in = sem("bias_in")
        b2_in = sem("b2_in")
        w_in = [sem(f"w_in{i}") for i in range(STAGES)]
        w_signed = sem("w_signed")
        w_summed = sem2("w_summed")
        w_turned = sem("w_turned")
        w_placed = sem("w_placed")
        table_loaded = sem("table_loaded")
        w_total = sem("w_total")
        w_totalled = sem("w_totalled")
        w_mean_step = sem("w_mean_step")
        w_mean_ready = sem("w_mean_ready")

        x_loaded = sem2("x_loaded")
        c_loaded = sem2("c_loaded")
        res_loaded = sem2("res_loaded")
        band_loaded = [sem2(f"band_loaded{i}_head") for i in range(2)]
        stored = sem2("stored")
        stats1_ready = sem("stats1_ready")
        mv1_step = sem("mv1_step")
        mv1_ready = sem("mv1_ready")
        rstd1_ready = sem("rstd1_ready")
        q_ready = sem("q_ready")
        q_turned = sem("q_turned")
        q_t_ready = sem("q_t_ready")
        c_turned = sem("c_turned")
        c_t_ready = sem("c_t_ready")
        prod_ready = sem2("prod_ready")
        c_squared = sem("c_squared")
        hi_ready = sem2("hi_ready")
        lo_ready = sem2("lo_ready")
        conv_ready = sem("conv_ready")
        z_ready = sem("z_ready")
        z_cleared = sem("z_cleared")
        fold_step = sem("fold_step")
        folded_ready = sem("folded_ready")
        sum_step = sem("sum_step")
        last_fold_step = sem("last_fold_step")
        last_sum_step = sem("last_sum_step")
        attn_ready = sem("attn_ready")
        attn_turned = sem("attn_turned")
        x1_ready = sem("x1_ready")
        x1_b2_ready = sem("x1_b2_ready")
        stats2_ready = sem("stats2_ready")
        mv2_step = sem("mv2_step")
        neg_mean2_ready = sem("neg_mean2_ready")
        cent_ready = sem("cent_ready")
        cmax_ready = sem("cmax_ready")
        var2_ready = sem("var2_ready")
        norm1_ready = sem("norm1_ready")
        scale1_step = sem("scale1_step")
        to_int1_ready = sem("to_int1_ready")
        unit1_ready = sem("unit1_ready")
        per_unit1_ready = sem("per_unit1_ready")
        factor_step = sem("factor_step")
        factors_ready = sem("factors_ready")
        xq_step = sem("xq_step")
        xq_ready = sem("xq_ready")
        xq_turned = sem("xq_turned")
        xq_t_ready = sem("xq_t_ready")
        first_ready = sem("first_ready")
        g_ready = sem("g_ready")
        squares_ready = sem("squares_ready")
        gmaxs_ready = sem("gmaxs_ready")
        gsum_ready = sem("gsum_ready")
        gmax_ready = sem("gmax_ready")
        gsum_step = sem("gsum_step")
        norm2_ready = sem("norm2_ready")
        scale2_step = sem("scale2_step")
        to_int2_ready = sem("to_int2_ready")
        unit2_ready = sem("unit2_ready")
        g_rounded = sem("g_rounded")
        half_rounded = sem("half_rounded")
        last_gq_t_ready = sem("last_gq_t_ready")
        gq_ready = sem("gq_ready")
        gq_turned = sem("gq_turned")
        gq_t_ready = sem("gq_t_ready")
        second_ready = sem("second_ready")
        y_scaled = sem("y_scaled")
        y_ready = sem("y_ready")
        last_y_ready = sem("last_y_ready")

        block = stack.enter_context(nc.Block())

        def pipeline(eng, iteration, drain):
            iteration(0, 0, True, True, False, False)
            iteration(0, 1, True, True, True, False)
            iteration(1, 0, True, True, True, True)
            iteration(1, 1, True, True, True, True)
            with eng.Fori(2, TILES // 2 - 1) as j:
                iteration(j, 0, True, True, True, True)
                iteration(j, 1, True, True, True, True)
            iteration(TILES // 2 - 1, 0, True, True, True, True)
            iteration(TILES // 2 - 1, 1, False, True, True, True)
            drain(TILES // 2 - 1)

        def products_of(half):
            base = half * 4 * EXT
            return (view(prod, half * 4 * NPR, [[NPR, 4], [CH8, HALF], [1, CH8]]),
                    view(c_ext, base + HALF * B, [[EXT, 4], [0, HALF], [1, CH8]]),
                    view(c_ext, base, [[EXT, 4], [B, HALF], [1, CH8]]))

        def sums_up_to(k):
            by_vector = min((k + 1) // 2, 6)
            return k + 1 - by_vector, by_vector

        def fold_rows(head):
            at = head * LB * ZS
            second = at + HALF * CH8
            return ((view(folded[head], 2 * CH8, [[FOLD, LB], [1, 2 * ROW]]),
                     view(z, second, [[ZS, LB], [1, 2 * ROW]]),
                     view(z, second + 2 * ROW, [[ZS, LB], [1, 2 * ROW]])),
                    (view(folded[head], 0, [[FOLD, LB], [1, 2 * CH8]]),
                     view(z, at, [[ZS, LB], [1, 2 * CH8]]),
                     view(z, at + 2 * CH8, [[ZS, LB], [1, 2 * CH8]])))

        def fold_folded(head):
            return ((view(folded[head], 2 * CH8, [[FOLD, LB], [1, ROW]]),
                     view(folded[head], 2 * CH8 + ROW, [[FOLD, LB], [1, ROW]])),
                    (view(folded[head], 0, [[FOLD, LB], [1, CH8]]),
                     view(folded[head], CH8, [[FOLD, LB], [1, CH8]])))

        def wrapped_slots(head):
            n = (HALF - 1) * B
            return (view(folded[head], CH8 - n, [[FOLD, LB], [1, n]]),
                    view(folded[head], 2 * CH8, [[FOLD, LB], [1, n]]))

        def both_sums(p, head):
            return (view(attn_t[p], head * CH8, [[P, LB], [1, CH8]]),
                    view(folded[head], 0, [[FOLD, LB], [1, CH8]]),
                    view(folded[head], 2 * CH8 + ROW - CH8, [[FOLD, LB], [1, CH8]]))

        def before(j, p, n):
            pair, parity = j - (n - p + 1) // 2, (p - n) % 2
            return pair, parity, 2 * pair + parity

        @block.sync
        def _(sp):
            def load_x_and_c(j, p, waits=True):
                t = 2 * j + p
                if waits:
                    sp.wait_ge(q_ready, t - 1)
                sp.dma_start(x_in[p][:], rows_of(x, t)).then_inc(x_loaded[p], 16)
                if waits:
                    sp.wait_ge(c_turned, t - 1)
                sp.dma_start(c_in[p][:], rows_of(ctx, t)).then_inc(c_loaded[p], 16)

            def load_band(j, p, waits=True):
                t = 2 * j + p
                if waits:
                    sp.wait_ge(conv_ready, 2 * LB * (t - 1))
                for head in range(2):
                    whole = kern_dram[0]
                    src = bass.AP(tensor=whole.tensor, offset=whole.offset + BAND * (2 * t + head),
                                  ap=[[1, P], [H * BAND, 2], [1, L]])
                    sp.dma_start(band[p][:, :, head].bitcast(F32), src).then_inc(band_loaded[p][head], 16)

            def load_residual(j, p, waits=True):
                t = 2 * j + p
                if waits:
                    sp.wait_ge(x1_ready, t - 1)
                sp.dma_start(x_res[p][:], rows_of(x, t)).then_inc(res_loaded[p], 16)

            def store(j, p, last=False):
                sp.wait_ge(last_y_ready if last else y_ready, p + 1 if last else 2 * j + p + 1)
                sp.dma_start(rows_of(out, 2 * j + p), y_out[p]).then_inc(stored[p], 16)

            w1_pairs = w1.rearrange("(k u p) n -> k p u n", u=2, p=P)
            w2_pairs = w2.rearrange("(r p) (k n) -> r k p n", p=P, n=2 * L)

            def load_weights(pairs):
                for k in pairs:
                    if k >= STAGES:
                        sp.wait_ge(w_signed, k + 1 - STAGES)
                        for engine in range(2):
                            if sums_up_to(k - STAGES)[engine] > sums_up_to(k - STAGES - 1)[engine]:
                                sp.wait_ge(w_summed[engine], sums_up_to(k - STAGES)[engine])
                    if k >= W_PAIRS:
                        src, dst = w2_pairs[(k - W_PAIRS) // 2, k % 2], w_stage[k % STAGES]
                    else:
                        src, dst = w1_pairs[k], w_stage[k % STAGES].rearrange("p (u n) -> p u n", n=L)
                    sp.dma_start(dst, src).then_inc(w_in[k % STAGES], 16)

            sp.dma_start(cent[0:H, :], ssm_kernel).then_inc(kern_in, 16)
            sp.dma_start(D_col[:], D.rearrange("(h a) -> h a", a=1)).then_inc(kern_in, 16)
            sp.dma_start(c_in[0][:], rows_of(ctx, 0)).then_inc(c_loaded[0], 16)
            sp.dma_start(x_in[0][:], rows_of(x, 0)).then_inc(x_loaded[0], 16)
            load_x_and_c(0, 1, False)
            load_weights(range(0, 1))
            sp.wait_ge(kern_split, 2)
            sp.dma_start(kern_dram[0], kern_hi.bitcast(F32)).then_inc(kern_stored, 16)
            sp.dma_start(kern_dram[1], kern_lo.bitcast(F32)).then_inc(kern_stored, 16)
            load_weights(range(1, 2))
            sp.wait_ge(kern_stored, 32)
            load_band(0, 0, False)
            load_weights(range(2, STAGES))
            sp.dma_start(b1_cols[:], b1.rearrange("(p n) -> p n", p=P)).then_inc(b1_in, 16)
            load_weights(range(4, 6))

            def iteration(j, p, prepare, convolve, first, second):
                if prepare and not (isinstance(j, int) and 2 * j + p == TILES - 2):
                    load_x_and_c(j + 1, p)
                if first and convolve:
                    pair, parity, _ = before(j, p, -1)
                    if not (isinstance(j, int) and 2 * j + p == TILES - 1):
                        load_band(pair, parity)
                        load_residual(pair, parity)
                if second and not (isinstance(j, int) and 2 * j + p == 2):
                    pair, parity, _ = before(j, p, 3)
                    store(pair, parity)

            load_weights(range(6, 10))
            load_x_and_c(1, 0)
            load_band(0, 1, False)
            load_weights(range(10, 11))
            sp.wait_ge(b1_step, 5)
            sp.dma_start(b1_dram.rearrange("j (p n) -> p j n", p=P), b1_parts[:]).then_inc(b1_stored, 16)
            load_weights(range(11, 14))
            load_residual(0, 0, False)
            load_weights(range(14, 16))
            sp.dma_start(b2_all[:], b2.rearrange("(a n) -> a n", a=1).to_broadcast([P, L])
                         ).then_inc(b2_in, 16)
            sp.wait_ge(b1_stored, 16)
            sp.wait_ge(pads_set, 5)
            for k in range(3):
                sp.dma_start(bias_rows[3 * k:3 * k + 3, :], b1_dram).then_inc(bias_in, 16)
            load_residual(0, 1, False)
            load_x_and_c(1, 1)
            load_band(1, 0)
            load_residual(1, 0)
            iteration(1, 0, True, True, True, True)
            iteration(1, 1, True, True, True, True)
            with sp.Fori(2, TILES // 2 - 1) as j:
                iteration(j, 0, True, True, True, True)
                iteration(j, 1, True, True, True, True)
            iteration(TILES // 2 - 1, 0, True, True, True, True)
            iteration(TILES // 2 - 1, 1, False, True, True, True)
            store(TILES // 2 - 2, 1)
            store(TILES // 2 - 1, 0, last=True)
            store(TILES // 2 - 1, 1, last=True)
            for p in range(2):
                sp.wait_ge(stored[p], 16 * TILES // 2)

        @block.tensor
        def _(pe):
            def turn_c(j, p):
                t = 2 * j + p
                pe.wait_ge(c_loaded[p], 16 * j + 16)
                pe.wait_ge(q_t_ready, t)
                for lb in range(LB):
                    last = nc.tensor.transpose(ps_t[:, lb * P:(lb + 1) * P],
                                               c_in[p][:, lb * P:(lb + 1) * P], ident[:])
                last.then_inc(c_turned, 1)

            def turn_q(j, p, others):
                t = 2 * j + p
                pe.wait_ge(q_ready, t + 1)
                pe.wait_ge(c_t_ready, 2 * t + 2)
                if others:
                    pe.wait_ge(x1_ready, t - 1)
                for lb in range(LB):
                    last = nc.tensor.transpose(ps_t[:, lb * P:(lb + 1) * P],
                                               q_rev[:, lb * P:(lb + 1) * P], ident[:])
                last.then_inc(q_turned, 1)

            def convolve_head(j, p, head, blocks=range(LB)):
                t = 2 * j + p
                if blocks[0] == 0:
                    pe.wait_ge(band_loaded[p][head], 16 * j + 16)
                for lb in blocks:
                    if head == 0 and lb % 2 == 0:
                        pe.wait_ge(hi_ready[lb // 2], t + 1)
                        pe.wait_ge(lo_ready[lb // 2], t + 1)
                    if head == 1 or not (isinstance(j, int) and t == 0):
                        pe.wait_ge(z_ready, 2 * LB * t + head * LB + lb - LB + 1)
                    n = 0
                    for mb in range(lb + 1):
                        at = (LB - 1 - (lb - mb)) * P
                        for kpart, ppart in ((0, 0), (0, 1), (1, 0)):
                            src = (prod_hi, prod_lo)[ppart][p]
                            last = nc.tensor.matmul(ps_y[lb][:, 0:NPR],
                                                    band[p][:, kpart, head, at:at + P],
                                                    src[:, mb, head, :],
                                                    start=(n == 0), stop=(n == 3 * lb + 2))
                            n += 1
                    last.then_inc(conv_ready, 1)

            def turn_attention(j, p, others):
                t = 2 * j + p
                pe.wait_ge(attn_ready, 2 * t + 2)
                if others:
                    pe.wait_ge(c_t_ready, 2 * t + 6)
                else:
                    pe.wait_ge(q_t_ready, TILES)
                    pe.wait_ge(x1_ready, t)
                for lb in range(LB):
                    last = nc.tensor.transpose(ps_t[:, lb * P:(lb + 1) * P],
                                               attn_t[p][:, lb, :], ident[:])
                last.then_inc(attn_turned, 1)

            def turn_tokens(j, p, others):
                t = 2 * j + p
                pe.wait_ge(xq_ready, t + 1)
                pe.wait_ge(factors_ready, t + 1)
                if others:
                    pe.wait_ge(gq_t_ready, 2 * t)
                for kb in range(LB + 1):
                    last = nc.tensor.transpose(ps_b[:, kb * P:(kb + 1) * P],
                                               xq[:, kb * P:(kb + 1) * P], ident_bf[:])
                last.then_inc(xq_turned, 1)

            def first_product(j, p, others, chunks=range(NCH)):
                t = 2 * j + p
                pe.wait_ge(xq_t_ready, t + 1)
                for n in chunks:
                    bank = ps_f[(p + n) % 2]
                    if n == 0 and others:
                        pe.wait_ge(g_ready, NCH * t)
                    if n == 1 and others:
                        pe.wait_ge(y_scaled, t)
                    if n >= 2:
                        pe.wait_ge(g_ready, NCH * t + n - 1)
                    for kb in range(LB):
                        nc.tensor.matmul(bank[:], xq_t[:, kb, :], w1s[:, kb, n * L:(n + 1) * L],
                                         start=(kb == 0), stop=False)
                    nc.tensor.matmul(bank[:], xq_t[:, LB, :], bias_rows[:, n * L:(n + 1) * L],
                                     start=False, stop=True).then_inc(first_ready, 1)

            def turn_g(j, p, half):
                t = 2 * j + p
                pe.wait_ge(gq_ready, 2 * t + half + 1)
                if half == 0:
                    pe.wait_ge(xq_t_ready, t + 1)
                else:
                    pe.wait_ge(gq_t_ready, 2 * t + 1)
                for k in range(KB // 2):
                    kb = half * KB // 2 + k
                    last = nc.tensor.transpose(ps_b[:, k * P:(k + 1) * P],
                                               gq[:, kb * P:(kb + 1) * P], ident_bf[:])
                last.then_inc(gq_turned, 1)

            def second_product(j, p, blocks):
                t = 2 * j + p
                bank = ps_f[p]
                if blocks[0] == 0:
                    pe.wait_ge(gq_t_ready, 2 * t + 1)
                    pe.wait_ge(g_ready, NCH * t + 3)
                for kb in blocks:
                    if kb == KB // 2:
                        pe.wait_ge(gq_t_ready, 2 * t + 2)
                    last = nc.tensor.matmul(bank[:], gq_t[:, kb, :], w2s[:, kb, :],
                                            start=(kb == 0), stop=(kb == KB - 1))
                if blocks[-1] == KB - 1:
                    last.then_inc(second_ready, 1)

            pe.wait_ge(pads_set, 2)
            turn_c(0, 0)
            turn_q(0, 0, False)
            def turn_weights(pairs):
                for k in pairs:
                    pe.wait_ge(w_signed, k + 1)
                    if k >= W_BANKS:
                        pe.wait_ge(w_placed, k + 1 - W_BANKS)
                    for i in range(8):
                        last = nc.tensor.transpose(w_bank[k % W_BANKS][:, i * P:(i + 1) * P],
                                                   w_sign[k % SIGNS][:, i * P:(i + 1) * P], ident_bf[:])
                    last.then_inc(w_turned, 1)

            def total_weights():
                pe.wait_ge(w_placed, 2 * W_PAIRS)
                pe.wait_ge(w_total, 1)
                nc.tensor.matmul(ps_f[0][:, 0:2], ones[:], abs_sum[:], start=True, stop=True
                                 ).then_inc(w_totalled, 1)

            def iteration(j, p, prepare, convolve, first, second):
                now, one, two_, nxt = (before(j, p, n)[:2] for n in (0, 1, 2, -1))
                start = 2 * j + p if isinstance(j, int) else 99
                if prepare:
                    turn_c(*nxt)
                if convolve:
                    convolve_head(*now, 0, range(0, 2))
                if start < 2:
                    turn_weights(range(0, 1) if start == 0 else range(10, 12))
                if convolve:
                    convolve_head(*now, 0, range(2, 3))
                if start == 1:
                    turn_attention(*one, prepare)
                if start < 2:
                    turn_weights(range(1, 3) if start == 0 else range(12, 14))
                if convolve:
                    convolve_head(*now, 0, range(3, LB))
                if start == 1:
                    turn_weights(range(14, 16))
                if first and start != 1:
                    turn_attention(*one, prepare)
                if start == 0:
                    turn_weights(range(3, 5))
                if convolve:
                    convolve_head(*now, 1, range(0, 2))
                if start == 1:
                    total_weights()
                if start == 0:
                    turn_weights(range(5, 7))
                if second:
                    turn_g(*two_, 0)
                if convolve:
                    convolve_head(*now, 1, range(2, 3))
                if start == 0:
                    turn_weights(range(7, 8))
                if second:
                    turn_g(*two_, 1)
                if second:
                    second_product(*two_, range(0, KB // 2))
                if convolve:
                    convolve_head(*now, 1, range(3, LB))
                if start == 0:
                    turn_weights(range(8, 10))
                if second:
                    second_product(*two_, range(KB // 2, KB - 2))
                if first:
                    turn_tokens(*one, second)
                if second:
                    second_product(*two_, range(KB - 2, KB))
                if prepare:
                    turn_q(*nxt, first)
                if start == 1:
                    pe.wait_ge(pads_set, 5)
                    pe.wait_ge(bias_in, 48)
                    pe.wait_ge(w_mean_ready, 1)
                if first and prepare:
                    first_product(*one, second)

            def first_product_last(j, chunks):
                for n in chunks:
                    for kb in range(LB):
                        nc.tensor.matmul(ps_y[n][:], xq_t[:, kb, :], w1s[:, kb, n * L:(n + 1) * L],
                                         start=(kb == 0), stop=False)
                    nc.tensor.matmul(ps_y[n][:], xq_t[:, LB, :], bias_rows[:, n * L:(n + 1) * L],
                                     start=False, stop=True).then_inc(first_ready, 1)

            def turn_g_last(j, p):
                t = 2 * j + p
                for n, half, bank in ((0, 1, ps_b), (1, 0, ps_b2)):
                    pe.wait_ge(gq_ready, 2 * t + n + 1)
                    if p == 0 and n == 0:
                        pe.wait_ge(xq_t_ready, TILES)
                    elif p == 0:
                        pe.wait_ge(x1_ready, TILES)
                    else:
                        pe.wait_ge(last_gq_t_ready, n + 1)
                    for k in range(KB // 2):
                        kb = half * KB // 2 + k
                        last = nc.tensor.transpose(bank[:, k * P:(k + 1) * P],
                                                   gq[:, kb * P:(kb + 1) * P], ident_bf[:])
                    last.then_inc(gq_turned, 1)

            def drain(j):
                t = 2 * j + 1
                first_product(j, 0, True, range(0, 3))
                turn_attention(j, 1, False)
                first_product(j, 0, True, range(3, NCH))
                pe.wait_ge(xq_ready, t + 1)
                pe.wait_ge(factors_ready, t + 1)
                pe.wait_ge(xq_t_ready, t)
                for kb in range(LB + 1):
                    last = nc.tensor.transpose(ps_b[:, kb * P:(kb + 1) * P],
                                               xq[:, kb * P:(kb + 1) * P], ident_bf[:])
                last.then_inc(xq_turned, 1)
                pe.wait_ge(z_ready, 2 * LB * (t + 1))
                pe.wait_ge(xq_t_ready, t + 1)
                first_product_last(j, range(NCH))
                turn_g_last(j, 0)
                for p in range(2):
                    t = 2 * j + p
                    if p == 1:
                        turn_g_last(j, 1)
                    pe.wait_ge(g_ready, NCH * (t + 1 - p))
                    for n, half in ((0, 1), (1, 0)):
                        if p == 1 and n == 1:
                            pe.wait_ge(gq_t_ready, 2 * (TILES - 2) + 1)
                        else:
                            pe.wait_ge(last_gq_t_ready, 2 * p + n + 1)
                        for k in range(KB // 2):
                            kb = half * KB // 2 + k
                            last = nc.tensor.matmul(ps_f[p][:], gq_t[:, kb, :], w2s[:, kb, :],
                                                    start=(n == 0 and k == 0), stop=(n == 1 and k == KB // 2 - 1))
                    last.then_inc(second_ready, 1)

            pipeline(pe, iteration, drain)

        @block.scalar
        def _(act):
            def extended(ext):
                n = HALF * B
                return ((view(ext, n, [[EXT, 2 * LB], [1, CH8]]), view(ps_t, 0, [[CH8, 2 * LB], [1, CH8]])),
                        (view(ext, 0, [[EXT, 2 * LB], [1, n]]), view(ps_t, CH8 - n, [[CH8, 2 * LB], [1, n]])))

            def place_c(j, p):
                t = 2 * j + p
                act.wait_ge(c_turned, t + 1)
                act.wait_ge(prod_ready[0], t)
                act.wait_ge(prod_ready[1], t)
                for dst, src in extended(c_ext):
                    nc.scalar.activation(dst, src, ACT.Copy).then_inc(c_t_ready, 1)

            def square_c(j, p):
                t = 2 * j + p
                act.wait_ge(c_t_ready, 2 * t + 1)
                act.wait_ge(lo_ready[0], t)
                act.wait_ge(lo_ready[1], t)
                nc.scalar.activation(view(prod, HALF * CH8, [[NPR, 2 * LB], [1, CH8]]),
                                     view(c_ext, HALF * B, [[EXT, 2 * LB], [1, CH8]]),
                                     ACT.Square).then_inc(c_squared, 1)

            def place_q(j, p, reuse):
                t = 2 * j + p
                act.wait_ge(q_turned, t + 1)
                if reuse:
                    act.wait_ge(z_ready, 2 * LB * (t - 1))
                (dst, src), (dst_wrapped, src_wrapped) = extended(q_ext[p])
                nc.scalar.activation(dst, src, ACT.Copy)
                nc.scalar.activation(dst_wrapped, src_wrapped, ACT.Copy).then_inc(q_t_ready, 1)

            def round_products(j, p, half, reuse):
                t = 2 * j + p
                act.wait_ge(prod_ready[half], t + 1)
                act.wait_ge(c_squared, t + 1)
                if half == 0 and reuse:
                    act.wait_ge(conv_ready, 2 * LB * (t - 1))
                nc.scalar.activation(prod_hi[p][:, 2 * half:2 * half + 2], prod[:, 2 * half:2 * half + 2],
                                     ACT.Copy).then_inc(hi_ready[half], 1)

            def centre(j, p):
                t = 2 * j + p
                act.wait_ge(neg_mean2_ready, t + 1)
                act.wait_ge(xq_ready, t)
                nc.scalar.activation(cent[:], x1[p][:], ACT.Identity, bias=neg_mean2[p][:]).then_inc(cent_ready, 1)

            def bias_factors(j, p, others):
                t = 2 * j + p
                act.wait_ge(per_unit1_ready, t + 1)
                if others:
                    act.wait_ge(xq_turned, t)
                for part in range(3):
                    left = per_unit1[p][:, part:part + 1]
                    factor = xq[:, L + 3 * part:L + 3 * part + 3]
                    if part < 2:
                        nc.scalar.activation(factor, left.to_broadcast([P, 3]), ACT.Copy).then_inc(factor_step, 1)
                        act.wait_ge(factor_step, 4 * t + 2 * part + 1)
                        nc.scalar.activation(per_unit1[p][:, part + 1:part + 2], factor[:, 0:1], ACT.Identity,
                                             bias=left, scale=-1.0).then_inc(factor_step, 1)
                        act.wait_ge(factor_step, 4 * t + 2 * part + 2)
                    else:
                        nc.scalar.activation(factor, left.to_broadcast([P, 3]), ACT.Copy).then_inc(factors_ready, 1)

            def place_tokens(j, p, others):
                t = 2 * j + p
                act.wait_ge(xq_turned, t + 1)
                if others:
                    act.wait_ge(first_ready, NCH * t)
                nc.scalar.activation(xq_t[:].rearrange("p a b -> p (a b)"), ps_b[:, 0:(LB + 1) * P],
                                     ACT.Copy).then_inc(xq_t_ready, 1)

            def scale_output(j, p, reuse):
                t = 2 * j + p
                act.wait_ge(second_ready, t + 1)
                act.wait_ge(unit2_ready, t + 1)
                if reuse:
                    act.wait_ge(stored[p], 16 * j)
                nc.scalar.activation(y_out[p], ps_f[p][:], ACT.Copy, scale=unit2[p][:]).then_inc(y_scaled, 1)

            def gelu(j, p, others, n, g=g):
                t = 2 * j + p
                if n == 0:
                    if others:
                        act.wait_ge(gq_ready, 2 * t)
                    act.wait_ge(unit1_ready, t + 1)
                act.wait_ge(first_ready, NCH * t + n + 1)
                bank = ps_y[n] if g is g_last else ps_f[(p + n) % 2]
                nc.scalar.activation(g[:, n * L:(n + 1) * L], bank[:], ACT.Gelu, scale=unit1[p][:]
                                     ).then_inc(g_ready, 1)

            def square(j, p, n, g=g):
                t = 2 * j + p
                act.wait_ge(g_ready, NCH * t + n + 1)
                if not (isinstance(j, int) and t == 0 and n < 2):
                    act.wait_ge(squares_ready, NCH * t + n - 1)
                nc.scalar.activation(square_dump[:, n % 2], g[:, n * L:(n + 1) * L], ACT.Square,
                                     accum_out=gsums[p][:, n:n + 1]).then_inc(squares_ready, 1)

            def gelu_and_squares(j, p, others):
                gelu(j, p, others, 0)
                for n in range(1, NCH):
                    gelu(j, p, others, n)
                    square(j, p, n - 1)
                square(j, p, NCH - 1)

            def round_g(j, p, half, g=g):
                t = 2 * j + p
                if half == 0:
                    act.wait_ge(to_int2_ready, t + 1)
                part = g[:, half * INNER // 2:(half + 1) * INNER // 2]
                nc.scalar.activation(part, part, ACT.Identity, bias=magic[:], scale=to_int2[p][:]
                                     ).then_inc(g_rounded, 1)

            def place_g(j, p, half, others):
                t = 2 * j + p
                act.wait_ge(gq_turned, 2 * t + half + 1)
                if half == 0 and others:
                    act.wait_ge(second_ready, t)
                nc.scalar.activation(gq_t[:, half * KB // 2:(half + 1) * KB // 2, :].rearrange("p a b -> p (a b)"),
                                     ps_b[:], ACT.Copy).then_inc(gq_t_ready, 1)

            place_c(0, 0)
            square_c(0, 0)
            round_products(0, 0, 0, False)
            place_q(0, 0, False)
            round_products(0, 0, 1, False)
            act.wait_ge(kern_stored, 32)

            def sign_weights(pairs):
                for k in pairs:
                    act.wait_ge(w_in[k % STAGES], 16 * (k // STAGES + 1))
                    if k >= SIGNS:
                        act.wait_ge(w_turned, k + 1 - SIGNS)
                    nc.scalar.activation(w_sign[k % SIGNS], w_stage[k % STAGES], ACT.Sign).then_inc(w_signed, 1)
                    if sums_up_to(k)[0] > sums_up_to(k - 1)[0]:
                        if k:
                            act.wait_ge(w_summed[0], sums_up_to(k - 1)[0])
                        m, n = k // W_PAIRS, k % W_PAIRS
                        nc.scalar.activation(w_dump[:], w_stage[k % STAGES], ACT.Abs,
                                             accum_out=abs_sums[:, m, n:n + 1]).then_inc(w_summed[0], 1)

            def iteration(j, p, prepare, convolve, first, second):
                now, one, two_, nxt = (before(j, p, n)[:2] for n in (0, 1, 2, -1))
                start = 2 * j + p if isinstance(j, int) else 99
                if start == 0:
                    sign_weights(range(0, 1))
                if prepare:
                    place_c(*nxt)
                    square_c(*nxt)
                if start < 2:
                    sign_weights(range(1, 5) if start == 0 else range(10, 16))
                if start == 1:
                    centre(*one)
                    nc.scalar.activation(gelu_first[:], magic[:], ACT.Gelu).then_inc(table_loaded, 1)
                if second:
                    round_g(*two_, 0)
                    round_g(*two_, 1)
                if second:
                    place_g(*two_, 0, start != 2)
                if prepare:
                    round_products(*nxt, 0, first)
                if start == 0:
                    sign_weights(range(5, 7))
                if first and start != 1:
                    centre(*one)
                if second:
                    place_g(*two_, 1, True)
                if prepare:
                    round_products(*nxt, 1, first)
                if start == 0:
                    sign_weights(range(7, 10))
                if first:
                    bias_factors(*one, second)
                    place_tokens(*one, second)
                if second:
                    scale_output(*two_, start > 3)
                if prepare:
                    place_q(*nxt, first)
                if first and prepare:
                    gelu_and_squares(*one, second)

            def place_last_half(j, p):
                t = 2 * j + p
                act.wait_ge(gq_turned, 2 * t + 2)
                act.wait_ge(second_ready, t)
                nc.scalar.activation(gq_t[:, 0:KB // 2, :].rearrange("p a b -> p (a b)"),
                                     ps_b2, ACT.Copy).then_inc(gq_t_ready, 1)

            def drain(j):
                gelu_and_squares(j, 0, True)
                bias_factors(j, 1, True)
                place_tokens(j, 1, True)
                act.wait_ge(folded_ready, 2 * TILES - 1)
                act.wait_ge(last_fold_step, 2)
                round_g(j, 0, 0)
                gelu(j, 1, False, 0, g_last)
                gelu(j, 1, False, 1, g_last)
                square(j, 1, 0, g_last)
                gelu(j, 1, False, 2, g_last)
                square(j, 1, 1, g_last)
                gelu(j, 1, False, 3, g_last)
                square(j, 1, 2, g_last)
                square(j, 1, 3, g_last)
                round_g(j, 1, 0, g_last)
                place_last_half(j, 1)

            pipeline(act, iteration, drain)

        @block.gpsimd
        def _(pool):
            pe_ = nc.gpsimd

            def make_rstd1(j, p):
                t = 2 * j + p
                pool.wait_ge(mv1_ready, t + 1)
                pe_.tensor_tensor(rstd1[p][:], var1[p][:], minus_half[:], ALU.pow).then_inc(rstd1_ready, 1)

            def multiply_c(j, p, half):
                t = 2 * j + p
                pool.wait_ge(c_t_ready, 2 * t + 2)
                if half == 0:
                    pool.wait_ge(hi_ready[0], t)
                    pool.wait_ge(hi_ready[1], t)
                    pool.wait_ge(lo_ready[0], t)
                    pool.wait_ge(lo_ready[1], t)
                pe_.tensor_tensor(*products_of(half), ALU.mult).then_inc(prod_ready[half], 1)

            def remainders(j, p, half):
                t = 2 * j + p
                pool.wait_ge(hi_ready[half], t + 1)
                at = slice(2 * half, 2 * half + 2)
                pe_.tensor_tensor(prod_lo[p][:, at], prod[:, at], prod_hi[p][:, at].bitcast(F32),
                                  ALU.subtract).then_inc(lo_ready[half], 1)

            def fold_last(j, p):
                t = 2 * j + p
                pool.wait_ge(z_ready, 2 * LB * t + LB)
                pool.wait_ge(attn_ready, 2 * t - 1)
                for into, one, other in fold_rows(0):
                    pe_.tensor_tensor(into, one, other, ALU.add).then_inc(last_fold_step, 1)
                for step, (into, other) in enumerate(fold_folded(0)):
                    pool.wait_ge(last_fold_step, 1 + step)
                    pe_.tensor_tensor(into, into, other, ALU.add).then_inc(last_fold_step, 1)

            def sum_head(j, p, head, reuse):
                t = 2 * j + p
                n = 4 * t + head
                if isinstance(j, int) and t == TILES - 1:
                    pool.wait_ge(last_fold_step, 4)
                else:
                    pool.wait_ge(folded_ready, 2 * t + head + 1)
                if head == 1:
                    for into, other in fold_folded(head):
                        pe_.tensor_tensor(into, into, other, ALU.add).then_inc(sum_step, 1)
                into, other = wrapped_slots(head)
                if head == 1:
                    pool.wait_ge(sum_step, n + 2)
                pe_.tensor_tensor(into, into, other, ALU.add).then_inc(sum_step, 1)
                pool.wait_ge(sum_step, n + 1 + 2 * head)
                if head == 0 and reuse:
                    pool.wait_ge(attn_turned, t - 1)
                pe_.tensor_tensor(*both_sums(p, head), ALU.add).then_inc(attn_ready, 1)

            def make_norm1(j, p):
                t = 2 * j + p
                pool.wait_ge(var2_ready, t + 1)
                pe_.tensor_tensor(norm1[p][:], var2[p][:], minus_half[:], ALU.pow).then_inc(norm1_ready, 1)

            def add_b2(j, p, reuse):
                t = 2 * j + p
                if isinstance(j, int) and t == 0:
                    pool.wait_ge(b2_in, 16)
                pool.wait_ge(x1_ready, t + 1)
                if reuse:
                    pool.wait_ge(y_ready, t - 1)
                pe_.tensor_tensor(x1_b2[p][:], x1[p][:], b2_all[:], ALU.add).then_inc(x1_b2_ready, 1)

            def output(j, p):
                t = 2 * j + p
                pool.wait_ge(y_scaled, t + 1)
                pool.wait_ge(x1_b2_ready, t + 1)
                pe_.tensor_tensor(y_out[p], y_out[p], x1_b2[p][:], ALU.add).then_inc(y_ready, 1)

            def make_norm2(j, p):
                t = 2 * j + p
                pool.wait_ge(gsum_ready, t + 1)
                pe_.tensor_tensor(gsum[p][:], gsum[p][:], inner_eps[:], ALU.add).then_inc(gsum_step, 1)
                pool.wait_ge(gsum_step, t + 1)
                pe_.tensor_tensor(norm2[p][:], gsum[p][:], minus_half[:], ALU.pow).then_inc(norm2_ready, 1)

            for m, value in ((ident, 0.0), (ones, 1.0), (magic, MAGIC), (minus_half, -0.5),
                             (inner_eps, INNER * 1e-6)):
                pe_.memset(m[:], value).then_inc(consts_set, 1)
            pool.wait_ge(consts_set, 5)
            pe_.affine_select(out=ident[:], in_=ident[:], compare_op=ALU.not_equal, fill=1.0, base=0,
                              pattern=[[-1, P]], channel_multiplier=1).then_inc(pads_set, 1)
            pool.wait_ge(pads_set, 1)
            pe_.tensor_copy(ident_bf[:], ident[:]).then_inc(pads_set, 1)
            pe_.memset(kern_rev[:, L:BAND], 0.0).then_inc(pads_set, 1)
            pe_.memset(bias_rows[:], 0.0).then_inc(pads_set, 1)
            pe_.memset(xq[:], 0.0).then_inc(pads_set, 1)
            make_rstd1(0, 0)
            multiply_c(0, 0, 1)
            remainders(0, 0, 1)

            def iteration(j, p, prepare, convolve, first, second):
                now, one, two_, nxt = (before(j, p, n)[:2] for n in (0, 1, 2, -1))
                if second:
                    make_norm2(*two_)
                if second and not (isinstance(j, int) and 2 * j + p == 2):
                    output(*before(j, p, 3)[:2])
                if prepare:
                    make_rstd1(*nxt)
                    multiply_c(*nxt, 0)
                    multiply_c(*nxt, 1)
                if first:
                    make_norm1(*one)
                if prepare:
                    remainders(*nxt, 0)
                if first:
                    add_b2(*one, not (isinstance(j, int) and 2 * j + p <= 2))
                if prepare:
                    remainders(*nxt, 1)
                if not prepare:
                    fold_last(*now)
                if convolve:
                    sum_head(*now, 0, not (isinstance(j, int) and 2 * j + p <= 1))
                if convolve and prepare:
                    sum_head(*now, 1, False)

            def drain(j):
                output(j - 1, 1)
                make_norm1(j, 1)
                add_b2(j, 1, True)
                make_norm2(j, 0)
                make_norm2(j, 1)

            pipeline(pool, iteration, drain)

        @block.vector
        def _(dve):
            v = nc.vector

            def stats1(j, p):
                dve.wait_ge(x_loaded[p], 16 * j + 16)
                v.bn_stats(stats1_buf[:], x_in[p][:]).then_inc(stats1_ready, 1)

            def mean1(j, p):
                v.bn_aggr(mv1[p][:], stats1_buf[:]).then_inc(mv1_step, 1)

            def variance1(j, p):
                dve.wait_ge(mv1_step, 2 * j + p + 1)
                v.tensor_scalar(var1[p][:], mv1[p][:, 1:2], 1e-5, None, ALU.add).then_inc(mv1_ready, 1)

            def make_q(j, p):
                t = 2 * j + p
                dve.wait_ge(rstd1_ready, t + 1)
                dve.wait_ge(q_turned, t)
                v.tensor_scalar(view(q_rev, 0, [[P, LB], [1, P]]), view(x_in[p], P - 1, [[P, LB], [-1, P]]),
                                mv1[p][:, 0:1], rstd1[p][:], ALU.subtract, ALU.mult).then_inc(q_ready, 1)

            def multiply_q(j, p, head, blocks, parts=range(2), prepare=False, first=False):
                t = 2 * j + p
                if prepare:
                    dve.wait_ge(stats1_ready, t + 2)
                if first:
                    dve.wait_ge(stats2_ready, t)
                for lb in blocks:
                    at = (head * LB + lb) * ZS
                    q_at = (lb * 2 + head) * EXT
                    if 0 in parts:
                        if head == 0 and lb == 0:
                            dve.wait_ge(q_t_ready, t + 1)
                        dve.wait_ge(conv_ready, 2 * LB * t + head * LB + lb + 1)
                        v.tensor_tensor(view(z, at, [[CH8, HALF], [1, CH8]]),
                                        view(ps_y[lb], 0, [[CH8, HALF], [1, CH8]]),
                                        view(q_ext[p], q_at, [[B, HALF], [1, CH8]]), ALU.mult)
                    if 1 in parts:
                        v.tensor_tensor(view(z, at + HALF * CH8, [[ROW + B, HALF], [1, CH8]]),
                                        view(ps_y[lb], CH8, [[CH8, HALF], [1, CH8]]),
                                        view(q_ext[p], q_at + HALF * B, [[0, HALF], [1, CH8]]),
                                        ALU.mult).then_inc(z_ready, 1)

            def fold(j, p, head, reuse):
                t = 2 * j + p
                dve.wait_ge(z_ready, 2 * LB * t + (head + 1) * LB)
                if reuse:
                    dve.wait_ge(attn_ready, 2 * t + head - 1)
                second, first = fold_rows(head)
                v.tensor_tensor(*second, ALU.add).then_inc(fold_step, 1)
                last = v.tensor_tensor(*first, ALU.add)
                last.then_inc(fold_step if head == 0 else folded_ready, 1)

            def fold_second_step(j, p):
                for step, (into, other) in enumerate(fold_folded(0)):
                    dve.wait_ge(fold_step, 3 * (2 * j + p) + 1 + step)
                    last = v.tensor_tensor(into, into, other, ALU.add)
                last.then_inc(folded_ready, 1)

            def residual(j, p, reuse):
                t = 2 * j + p
                dve.wait_ge(attn_turned, t + 1)
                dve.wait_ge(res_loaded[p], 16 * j + 16)
                if reuse:
                    dve.wait_ge(x1_b2_ready, t - 1)
                v.tensor_tensor(view(x1[p], 0, [[P, LB], [1, P]]), view(ps_t, P - 1, [[P, LB], [-1, P]]),
                                view(x_res[p], 0, [[P, LB], [1, P]]), ALU.add).then_inc(x1_ready, 1)

            def stats2(j, p):
                dve.wait_ge(x1_ready, 2 * j + p + 1)
                v.bn_stats(stats2_buf[:], x1[p][:]).then_inc(stats2_ready, 1)

            def variance2(j, p):
                t = 2 * j + p
                if isinstance(j, int):
                    dve.wait_ge(stats2_ready, t + 1)
                v.bn_aggr(mv2[p][:], stats2_buf[:]).then_inc(mv2_step, 1)
                dve.wait_ge(mv2_step, t + 1)
                v.tensor_scalar(neg_mean2[p][:], mv2[p][:, 0:1], -1.0, None, ALU.mult).then_inc(neg_mean2_ready, 1)
                v.tensor_scalar(var2[p][:], mv2[p][:, 1:2], L * (1 + 1e-6), L * 1e-5 * 1e-6, ALU.mult, ALU.add
                                ).then_inc(var2_ready, 1)

            def largest_centred(j, p):
                t = 2 * j + p
                dve.wait_ge(cent_ready, t + 1)
                v.tensor_reduce(cmax[p][:], cent[:], AX.X, ALU.max, apply_absolute_value=True
                                ).then_inc(cmax_ready, 1)

            def largest_normalised(largest, norm, step):
                v.tensor_scalar(biggest[:, 0:1], largest[:], norm[:], 1e-5, ALU.mult, ALU.max).then_inc(step, 1)

            def invert_largest(t, step):
                dve.wait_ge(step, 2 * t + 1)
                v.reciprocal(biggest[:, 1:2], biggest[:, 0:1]).then_inc(step, 1)

            def make_unit(unit, mean_of, unit_done):
                v.tensor_scalar(unit[:], biggest[:, 0:1], 1.0 / 127.0, mean_of, ALU.mult, ALU.mult
                                ).then_inc(unit_done, 1)

            def make_to_int(to_int, norm, to_int_done):
                v.tensor_scalar(to_int[:], biggest[:, 1:2], norm[:], 127.0, ALU.mult, ALU.mult
                                ).then_inc(to_int_done, 1)

            def largest_of_tokens(j, p):
                t = 2 * j + p
                dve.wait_ge(cmax_ready, t + 1)
                dve.wait_ge(norm1_ready, t + 1)
                largest_normalised(cmax[p], norm1[p], scale1_step)

            def scale_tokens(j, p):
                t = 2 * j + p
                invert_largest(t, scale1_step)
                dve.wait_ge(scale1_step, 2 * t + 2)
                v.tensor_scalar(per_unit1[p][:, 0:1], biggest[:, 1:2], 127.0, w_mean_inv[:, 0:1],
                                ALU.mult, ALU.mult).then_inc(per_unit1_ready, 1)
                make_to_int(to_int1[p], norm1[p], to_int1_ready)
                make_unit(unit1[p], w_mean[:, 0:1], unit1_ready)

            def quantise_tokens(j, p, others):
                t = 2 * j + p
                dve.wait_ge(to_int1_ready, t + 1)
                v.tensor_scalar(cent[:], cent[:], to_int1[p][:], MAGIC, ALU.mult, ALU.add).then_inc(xq_step, 1)
                dve.wait_ge(xq_step, t + 1)
                if others:
                    dve.wait_ge(xq_turned, t)
                v.tensor_scalar(xq[:, 0:L], cent[:], MAGIC, 127.0, ALU.subtract, ALU.min).then_inc(xq_ready, 1)

            def largest_g(j, p, chunks, g=g):
                t = 2 * j + p
                for n in chunks:
                    dve.wait_ge(g_ready, NCH * t + n + 1)
                    v.tensor_reduce(gmaxs[p][:, n:n + 1], g[:, n * L:(n + 1) * L], AX.X, ALU.max,
                                    apply_absolute_value=True).then_inc(gmaxs_ready, 1)

            def combine_g(j, p):
                t = 2 * j + p
                dve.wait_ge(gmaxs_ready, NCH * t + NCH)
                v.tensor_reduce(gmax[p][:], gmaxs[p][:], AX.X, ALU.max).then_inc(gmax_ready, 1)
                dve.wait_ge(squares_ready, NCH * t + NCH)
                v.tensor_reduce(gsum[p][:], gsums[p][:], AX.X, ALU.add).then_inc(gsum_ready, 1)

            def largest_of_g(j, p):
                t = 2 * j + p
                dve.wait_ge(gmax_ready, t + 1)
                dve.wait_ge(norm2_ready, t + 1)
                largest_normalised(gmax[p], norm2[p], scale2_step)

            def scale_g(j, p):
                t = 2 * j + p
                invert_largest(t, scale2_step)
                make_unit(unit2[p], w_mean[:, 1:2], unit2_ready)
                dve.wait_ge(scale2_step, 2 * t + 2)
                make_to_int(to_int2[p], norm2[p], to_int2_ready)

            def quantise_g(j, p, half, others):
                t = 2 * j + p
                dve.wait_ge(g_rounded, 2 * t + half + 1)
                if others and half == 0:
                    dve.wait_ge(gq_turned, 2 * t)
                at = slice(half * INNER // 2, (half + 1) * INNER // 2)
                v.tensor_scalar(gq[:, at], g[:, at], MAGIC, 127.0, ALU.subtract, ALU.min).then_inc(gq_ready, 1)

            def output_last(j, p):
                t = 2 * j + p
                dve.wait_ge(second_ready, t + 1)
                dve.wait_ge(x1_b2_ready, t + 1)
                dve.wait_ge(unit2_ready, t + 1)
                dve.wait_ge(stored[p], 16 * j)
                v.scalar_tensor_tensor(y_out[p], ps_f[p][:], unit2[p][:], x1_b2[p][:],
                                       ALU.mult, ALU.add).then_inc(last_y_ready, 1)

            def clear_slots(head):
                v.memset(view(z, head * LB * ZS + HALF * CH8, [[ZS, LB], [1, HALF * ROW]]), 0.0
                         ).then_inc(z_cleared, 1)

            dve.wait_ge(kern_in, 32)
            dve.wait_ge(pads_set, 3)
            v.tensor_copy(kern_rev[:, 0:L], cent[0:H, L - 1::-1]).then_inc(kern_step, 1)
            dve.wait_ge(kern_step, 1)
            v.tensor_tensor(kern_rev[:, L - 1:L], kern_rev[:, L - 1:L], D_col[:], ALU.add).then_inc(kern_step, 1)
            dve.wait_ge(kern_step, 2)
            v.tensor_copy(kern_hi, kern_rev[:]).then_inc(kern_split, 1)
            dve.wait_ge(kern_split, 1)
            v.tensor_tensor(kern_lo, kern_rev[:], kern_hi.bitcast(F32), ALU.subtract).then_inc(kern_split, 1)
            stats1(0, 0)
            dve.wait_ge(stats1_ready, 1)
            mean1(0, 0)
            variance1(0, 0)
            dve.wait_ge(c_t_ready, 2)
            v.tensor_tensor(*products_of(0), ALU.mult).then_inc(prod_ready[0], 1)
            make_q(0, 0)
            clear_slots(0)
            dve.wait_ge(hi_ready[0], 1)
            v.tensor_tensor(prod_lo[0][:, 0:2], prod[:, 0:2], prod_hi[0][:, 0:2].bitcast(F32),
                            ALU.subtract).then_inc(lo_ready[0], 1)

            def split_b1():
                dve.wait_ge(b1_in, 16)
                v.tensor_copy(b1_parts[:, 0], b1_cols[:]).then_inc(b1_step, 1)
                dve.wait_ge(b1_step, 1)
                v.tensor_tensor(b1_cols[:], b1_cols[:], b1_parts[:, 0], ALU.subtract).then_inc(b1_step, 1)
                dve.wait_ge(b1_step, 2)
                v.tensor_copy(b1_parts[:, 1], b1_cols[:]).then_inc(b1_step, 1)
                dve.wait_ge(b1_step, 3)
                v.tensor_tensor(b1_cols[:], b1_cols[:], b1_parts[:, 1], ALU.subtract).then_inc(b1_step, 1)
                dve.wait_ge(b1_step, 4)
                v.tensor_copy(b1_parts[:, 2], b1_cols[:]).then_inc(b1_step, 1)

            def place_weights(pairs):
                for k in pairs:
                    dve.wait_ge(w_turned, k + 1)
                    src = w_bank[k % W_BANKS]
                    if k >= W_PAIRS:
                        at = k % 2 * 8
                        block = (k - W_PAIRS) // 2
                        dst = w2s[:, at:at + 8, block * P:(block + 1) * P]
                        v.tensor_copy(dst, src.rearrange("p (c n) -> p c n", n=P)).then_inc(w_placed, 1)
                    else:
                        v.tensor_copy(view(w1s, 2 * k * P, [[P, 2], [INNER, LB], [1, P]]),
                                      src.rearrange("p (u c n) -> p u c n", u=2, n=P)).then_inc(w_placed, 1)

            def sum_weights(k):
                dve.wait_ge(w_in[k % STAGES], 16 * (k // STAGES + 1))
                m, n = k // W_PAIRS, k % W_PAIRS
                v.tensor_reduce(abs_sums[:, m, n:n + 1], w_stage[k % STAGES], AX.X, ALU.add,
                                apply_absolute_value=True).then_inc(w_summed[1], 1)

            def total_of_weights():
                for i in range(2):
                    dve.wait_ge(w_summed[i], sums_up_to(2 * W_PAIRS - 1)[i])
                v.tensor_reduce(abs_sum[:], abs_sums[:], AX.X, ALU.add).then_inc(w_total, 1)

            def mean_of_weights():
                dve.wait_ge(w_totalled, 1)
                v.tensor_scalar(w_mean[:], ps_f[0][:, 0:2], 1.0 / (INNER * L), TINY,
                                ALU.mult, ALU.max).then_inc(w_mean_step, 1)
                dve.wait_ge(w_mean_step, 1)
                v.reciprocal(w_mean_inv[:], w_mean[:]).then_inc(w_mean_ready, 1)

            def iteration(j, p, prepare, convolve, first, second):
                now, one, two_, nxt = (before(j, p, n)[:2] for n in (0, 1, 2, -1))
                start = 2 * j + p if isinstance(j, int) else 99
                if second:
                    largest_g(*two_, range(3, NCH))
                if prepare:
                    stats1(*nxt)
                if second:
                    combine_g(*two_)
                if start == 0:
                    dve.wait_ge(stats1_ready, 2)
                    mean1(*nxt)
                    variance1(*nxt)
                    clear_slots(1)
                    dve.wait_ge(z_cleared, 2)
                if convolve:
                    multiply_q(*now, 0, range(0, 1), prepare=prepare)
                if prepare and start > 0:
                    mean1(*nxt)
                if second:
                    largest_of_g(*two_)
                if prepare and start > 0:
                    variance1(*nxt)
                if start == 0:
                    sum_weights(1)
                if second:
                    scale_g(*two_)
                if convolve:
                    multiply_q(*now, 0, range(1, 2))
                if start == 1:
                    sum_weights(11)
                if start < 2:
                    place_weights(range(0, 1) if start == 0 else range(10, 12))
                if start == 0:
                    split_b1()
                if convolve:
                    multiply_q(*now, 0, range(2, 3))
                if start == 1:
                    residual(*one, False)
                    stats2(*one)
                    variance2(*one)
                if start < 2:
                    place_weights(range(1, 3) if start == 0 else range(12, 14))
                if start == 0:
                    sum_weights(3)
                if start == 1:
                    multiply_q(*now, 0, range(3, LB))
                    place_weights(range(14, 16))
                    total_of_weights()
                    largest_centred(*one)
                if second:
                    quantise_g(*two_, 0, start != 2)
                if first and start != 1:
                    residual(*one, start > 2)
                if second:
                    quantise_g(*two_, 1, True)
                if start == 1:
                    mean_of_weights()
                if convolve and start != 1:
                    multiply_q(*now, 0, range(3, LB), parts=range(0, 1))
                if first and start != 1:
                    stats2(*one)
                if convolve and start != 1:
                    multiply_q(*now, 0, range(3, LB), parts=range(1, 2), first=first)
                if first and start != 1:
                    variance2(*one)
                if start == 0:
                    make_q(*nxt)
                    place_weights(range(3, 5))
                    sum_weights(5)
                if convolve:
                    multiply_q(*now, 1, range(0, 1))
                if first and start != 1:
                    largest_centred(*one)
                if first:
                    multiply_q(*now, 1, range(1, 2), parts=range(0, 1))
                    largest_of_tokens(*one)
                    multiply_q(*now, 1, range(1, 2), parts=range(1, 2))
                    scale_tokens(*one)
                    quantise_tokens(*one, second)
                    if prepare:
                        make_q(*nxt)
                else:
                    multiply_q(*now, 1, range(1, 2))
                if start == 0:
                    place_weights(range(5, 7))
                    sum_weights(7)
                if convolve:
                    multiply_q(*now, 1, range(2, 3))
                if start == 0:
                    place_weights(range(7, 8))
                    sum_weights(9)
                if convolve and prepare:
                    fold(*now, 0, start > 0)
                    fold_second_step(*now)
                if convolve:
                    multiply_q(*now, 1, range(3, LB))
                if start == 0:
                    place_weights(range(8, 10))
                if convolve:
                    fold(*now, 1, start > 0)
                if first and prepare:
                    largest_g(*one, range(0, 3))

            def quantise_last(j, p, g):
                t = 2 * j + p
                middle = INNER // 2
                dve.wait_ge(to_int2_ready, t + 1)
                v.tensor_scalar(g[:, middle:], g[:, middle:], to_int2[p][:], MAGIC, ALU.mult, ALU.add
                                ).then_inc(half_rounded, 1)
                dve.wait_ge(gq_turned, 2 * t)
                dve.wait_ge(half_rounded, p + 1)
                v.tensor_scalar(gq[:, middle:], g[:, middle:], MAGIC, 127.0, ALU.subtract, ALU.min
                                ).then_inc(gq_ready, 1)
                dve.wait_ge(g_rounded, 2 * (TILES - 2) + p + 1)
                v.tensor_scalar(gq[:, :middle], g[:, :middle], MAGIC, 127.0, ALU.subtract, ALU.min
                                ).then_inc(gq_ready, 1)

            def place_half(j, p, half):
                t = 2 * j + p
                dve.wait_ge(gq_turned, 2 * t + 2 - half)
                dve.wait_ge(second_ready, t)
                v.tensor_copy(gq_t[:, half * KB // 2:(half + 1) * KB // 2, :].rearrange("p a b -> p (a b)"),
                              ps_b[:] if half else ps_b2).then_inc(last_gq_t_ready, 1)

            def drain(j):
                dve.wait_ge(folded_ready, 2 * TILES - 1)
                for into, other in fold_folded(1):
                    v.tensor_tensor(into, into, other, ALU.add).then_inc(last_sum_step, 1)
                into, other = wrapped_slots(1)
                dve.wait_ge(last_sum_step, 2)
                v.tensor_tensor(into, into, other, ALU.add).then_inc(last_sum_step, 1)
                dve.wait_ge(last_sum_step, 3)
                dve.wait_ge(attn_ready, 2 * TILES - 1)
                v.tensor_tensor(*both_sums(1, 1), ALU.add).then_inc(attn_ready, 1)
                largest_g(j, 0, range(0, 1))
                residual(j, 1, True)
                stats2(j, 1)
                variance2(j, 1)
                v.tensor_scalar(cent[:], x1[1][:], mv2[1][:, 0:1], None, ALU.subtract).then_inc(cent_ready, 1)
                largest_centred(j, 1)
                largest_of_tokens(j, 1)
                scale_tokens(j, 1)
                quantise_tokens(j, 1, True)
                largest_g(j, 0, range(1, NCH))
                combine_g(j, 0)
                largest_of_g(j, 0)
                scale_g(j, 0)
                quantise_last(j, 0, g)
                largest_g(j, 1, range(0, NCH - 1), g_last)
                place_half(j, 0, 1)
                largest_g(j, 1, range(NCH - 1, NCH), g_last)
                combine_g(j, 1)
                place_half(j, 0, 0)
                largest_of_g(j, 1)
                scale_g(j, 1)
                quantise_last(j, 1, g_last)
                place_half(j, 1, 1)
                output_last(j, 0)
                output_last(j, 1)

            pipeline(dve, iteration, drain)


_INS = ["x", "ctx_2048", "L0_xattn_ssm_kernel", "L0_xattn_D", "L0_ffn_w1", "L0_ffn_b1", "L0_ffn_w2", "L0_ffn_b2"]


def kernel(**inputs):
    import numpy as _np
    import concourse.bacc as _bacc
    from concourse.bass_utils import run_bass_kernel_spmd as _run

    nc = _bacc.Bacc("TRN2", target_bir_lowering=False, num_devices=1)
    arrays, args = {}, []
    for name in _INS:
        a = _np.ascontiguousarray(inputs[name])
        arrays[f"in_{name}"] = a
        args.append(nc.dram_tensor(f"in_{name}", a.shape, mybir.dt.from_np(a.dtype), kind="ExternalInput").ap())
    out = nc.dram_tensor("out", inputs["x"].shape, F32, kind="ExternalOutput").ap()
    build(nc, *args, out)
    return _run(nc, [arrays], core_ids=[0]).results[0]["out"]
```
